# Optimizing a Trainium2 kernel written in Bass

```python
import numpy as np
import jax
import jax.numpy as jnp

def _softmax(x, axis=-1):
    return jax.nn.softmax(x, axis=axis)

def _gelu(x):
    return jax.nn.gelu(x, approximate=True)

def _silu(x):
    return jax.nn.silu(x)

def _sigmoid(x):
    return jax.nn.sigmoid(x)

def _layernorm(x, axis=-1, eps=1e-05):
    m = jnp.mean(x, axis=axis, keepdims=True)
    v = jnp.var(x, axis=axis, keepdims=True)
    return (x - m) / jnp.sqrt(v + eps)

def _scatter_add(tgt, idx, src, axis=0):
    return tgt.at[idx].add(src)

def _segment_sum(src, seg, n):
    return jax.ops.segment_sum(src, seg, n)
kernel_name = 'mk_lm_tower_d1_tok_ids1024_r4_5d1fcb'

def setup_inputs(seed: int=0):
    np.random.seed(seed)
    _w = jnp.asarray

    def _rec_inputs():
        import jax
        import jax.numpy as jnp
        _rk = jax.random.key(seed)
        x = jax.random.randint(jax.random.fold_in(_rk, 1), (16, 128), 0, 31993, jnp.int32)
        return x
    x = _rec_inputs()

    def _L0_tok_setup():
        import jax, jax.numpy as jnp
        import numpy as np
        VOCAB = 8000
        DIM = 256
        BATCH = 4
        SEQ = 512
        key = jax.random.key(seed)
        k_ids, k_emb = jax.random.split(key)
        token_ids = jax.random.randint(k_ids, (BATCH, SEQ), 0, VOCAB, dtype=jnp.int32)
        embedding = jax.random.truncated_normal(k_emb, -3.0, 3.0, (VOCAB, DIM), dtype=jnp.float32)
        return {'token_ids': token_ids, 'embedding': embedding}
    _L0_tok_all = _L0_tok_setup()
    _L0_tok_in = {k: v for k, v in _L0_tok_all.items() if k in ('embedding',)}
    del _L0_tok_all

    def _L0_attn_setup():
        import jax, jax.numpy as jnp
        import numpy as np
        BATCH = 1
        SEQ = 512
        D_MODEL = 256
        D_STATE = 16
        D_CONV = 4
        EXPAND = 2
        D_INNER = EXPAND * D_MODEL
        DT_RANK = (D_MODEL + 15) // 16
        EPS = 1e-05
        key = jax.random.key(seed)
        ks = jax.random.split(key, 8)
        s = lambda k, shape, scale=0.02: jax.random.normal(k, shape, jnp.float32) * scale
        return {'x': jax.random.normal(ks[0], (BATCH, SEQ, D_MODEL), jnp.float32), 'ln_w': jnp.ones((D_MODEL,), jnp.float32), 'ln_b': jnp.zeros((D_MODEL,), jnp.float32), 'W_in': s(ks[1], (2 * D_INNER, D_MODEL)), 'conv_w': s(ks[2], (D_INNER, D_CONV), 0.1), 'conv_b': jnp.zeros((D_INNER,), jnp.float32), 'W_xproj': s(ks[3], (DT_RANK + 2 * D_STATE, D_INNER)), 'W_dt': s(ks[4], (D_INNER, DT_RANK), 0.1), 'b_dt': s(ks[5], (D_INNER,), 0.1), 'A_log': jnp.log(jnp.broadcast_to(jnp.arange(1, D_STATE + 1, dtype=jnp.float32), (D_INNER, D_STATE))), 'Dskip': jnp.ones((D_INNER,), jnp.float32), 'W_out': s(ks[6], (D_MODEL, D_INNER))}
    _L0_attn_all = _L0_attn_setup()
    _L0_attn_in = {k: v for k, v in _L0_attn_all.items() if k in ('ln_w', 'ln_b', 'W_in', 'conv_w', 'conv_b', 'W_xproj', 'W_dt', 'b_dt', 'A_log', 'Dskip', 'W_out')}
    del _L0_attn_all

    def _L0_ffn_setup():
        import jax, jax.numpy as jnp
        import numpy as np
        N_EMBD = 256
        NUM_EXPERTS = 8
        TOP_K = 2

        def new_gelu(x):
            c = jnp.sqrt(2.0 / jnp.pi).astype(x.dtype)
            return 0.5 * x * (1.0 + jnp.tanh(c * (x + 0.044715 * x ** 3)))
        key = jax.random.key(seed)
        ks = jax.random.split(key, 6)
        C, E, H = (N_EMBD, NUM_EXPERTS, 4 * N_EMBD)
        x = jax.random.normal(ks[0], (4, 512, C), dtype=jnp.float32)
        router_w = 0.02 * jax.random.normal(ks[1], (E, C), dtype=jnp.float32)
        w1 = 0.02 * jax.random.normal(ks[2], (E, H, C), dtype=jnp.float32)
        b1 = jnp.zeros((E, H), dtype=jnp.float32)
        w2 = 0.02 * jax.random.normal(ks[3], (E, C, H), dtype=jnp.float32)
        b2 = jnp.zeros((E, C), dtype=jnp.float32)
        return {'x': x, 'router_w': router_w, 'w1': w1, 'b1': b1, 'w2': w2, 'b2': b2}
    _L0_ffn_all = _L0_ffn_setup()
    _L0_ffn_in = {k: v for k, v in _L0_ffn_all.items() if k in ('router_w', 'w1', 'b1', 'w2', 'b2')}
    del _L0_ffn_all
    return {'x': x, 'L0_tok_embedding': _L0_tok_in['embedding'], 'L0_attn_ln_w': _L0_attn_in['ln_w'], 'L0_attn_ln_b': _L0_attn_in['ln_b'], 'L0_attn_W_in': _L0_attn_in['W_in'], 'L0_attn_conv_w': _L0_attn_in['conv_w'], 'L0_attn_conv_b': _L0_attn_in['conv_b'], 'L0_attn_W_xproj': _L0_attn_in['W_xproj'], 'L0_attn_W_dt': _L0_attn_in['W_dt'], 'L0_attn_b_dt': _L0_attn_in['b_dt'], 'L0_attn_A_log': _L0_attn_in['A_log'], 'L0_attn_Dskip': _L0_attn_in['Dskip'], 'L0_attn_W_out': _L0_attn_in['W_out'], 'L0_ffn_router_w': _L0_ffn_in['router_w'], 'L0_ffn_w1': _L0_ffn_in['w1'], 'L0_ffn_b1': _L0_ffn_in['b1'], 'L0_ffn_w2': _L0_ffn_in['w2'], 'L0_ffn_b2': _L0_ffn_in['b2']}

def reference(x, L0_tok_embedding, L0_attn_ln_w, L0_attn_ln_b, L0_attn_W_in, L0_attn_conv_w, L0_attn_conv_b, L0_attn_W_xproj, L0_attn_W_dt, L0_attn_b_dt, L0_attn_A_log, L0_attn_Dskip, L0_attn_W_out, L0_ffn_router_w, L0_ffn_w1, L0_ffn_b1, L0_ffn_w2, L0_ffn_b2):
    import jax
    import jax.numpy as jnp

    def _L0_tok_ref(token_ids, embedding):
        import jax, jax.numpy as jnp
        import numpy as np
        VOCAB = 8000
        DIM = 256
        BATCH = 4
        SEQ = 512
        one_hot = jax.nn.one_hot(token_ids, VOCAB, dtype=embedding.dtype)
        return jnp.einsum('bsv,vd->bsd', one_hot, embedding)

    def _L0_attn_ref(x, ln_w, ln_b, W_in, conv_w, conv_b, W_xproj, W_dt, b_dt, A_log, Dskip, W_out):
        import jax, jax.numpy as jnp
        import numpy as np
        BATCH = 1
        SEQ = 512
        D_MODEL = 256
        D_STATE = 16
        D_CONV = 4
        EXPAND = 2
        D_INNER = EXPAND * D_MODEL
        DT_RANK = (D_MODEL + 15) // 16
        EPS = 1e-05
        residual = x
        mu = x.mean(-1, keepdims=True)
        var = x.var(-1, keepdims=True)
        xn = (x - mu) * jax.lax.rsqrt(var + EPS) * ln_w + ln_b
        xz = jnp.einsum('bld,ed->ble', xn, W_in)
        xc, z = jnp.split(xz, 2, axis=-1)
        L = xc.shape[1]
        xpad = jnp.pad(xc, ((0, 0), (D_CONV - 1, 0), (0, 0)))
        xconv = conv_b
        for k in range(D_CONV):
            xconv = xconv + xpad[:, k:k + L, :] * conv_w[:, k]
        xconv = jax.nn.silu(xconv)
        proj = jnp.einsum('bld,ed->ble', xconv, W_xproj)
        dt, Bm, Cm = jnp.split(proj, [DT_RANK, DT_RANK + D_STATE], axis=-1)
        dt = jax.nn.softplus(jnp.einsum('blr,dr->bld', dt, W_dt) + b_dt)
        A = -jnp.exp(A_log)
        deltaA = jnp.exp(dt[..., None] * A)
        deltaBu = dt[..., None] * Bm[:, :, None, :] * xconv[..., None]

        def combine(c1, c2):
            a1, b1 = c1
            a2, b2 = c2
            return (a2 * a1, a2 * b1 + b2)
        _, h = jax.lax.associative_scan(combine, (deltaA, deltaBu), axis=1)
        y = jnp.einsum('bldn,bln->bld', h, Cm) + xconv * Dskip
        y = y * jax.nn.silu(z)
        out = jnp.einsum('bld,od->blo', y, W_out)
        return out + residual

    def _L0_ffn_ref(x, router_w, w1, b1, w2, b2):
        import jax, jax.numpy as jnp
        import numpy as np
        N_EMBD = 256
        NUM_EXPERTS = 8
        TOP_K = 2

        def new_gelu(x):
            c = jnp.sqrt(2.0 / jnp.pi).astype(x.dtype)
            return 0.5 * x * (1.0 + jnp.tanh(c * (x + 0.044715 * x ** 3)))
        B, T, C = x.shape
        E = router_w.shape[0]
        x_flat = x.reshape(B * T, C)
        router_logits = x_flat @ router_w.T
        router_probs = jax.nn.softmax(router_logits, axis=-1)
        top_k_probs, top_k_idx = jax.lax.top_k(router_probs, TOP_K)
        top_k_probs = top_k_probs / (top_k_probs.sum(axis=-1, keepdims=True) + 1e-08)
        cw = (jax.nn.one_hot(top_k_idx, E, dtype=x.dtype) * top_k_probs[..., None]).sum(axis=1)
        output = jnp.zeros_like(x_flat)
        for e in range(E):
            h = new_gelu(x_flat @ w1[e].T + b1[e])
            out_e = h @ w2[e].T + b2[e]
            output = output + cw[:, e:e + 1] * out_e
        return output.reshape(B, T, C)
    h = _L0_tok_ref(x, L0_tok_embedding)
    h = h + _L0_attn_ref(_layernorm(h, axis=-1), L0_attn_ln_w, L0_attn_ln_b, L0_attn_W_in, L0_attn_conv_w, L0_attn_conv_b, L0_attn_W_xproj, L0_attn_W_dt, L0_attn_b_dt, L0_attn_A_log, L0_attn_Dskip, L0_attn_W_out)
    h = h + _L0_ffn_ref(_layernorm(h, axis=-1), L0_ffn_router_w, L0_ffn_w1, L0_ffn_b1, L0_ffn_w2, L0_ffn_b2)
    return h

_drawn_inputs = setup_inputs


def setup_inputs(seed=0):
    import zlib

    import numpy as np

    out = dict(_drawn_inputs(seed))
    spreads = {'L0_attn_ln_w': (1.0, 0.6),
     'L0_attn_ln_b': (0.0, 0.1),
     'L0_attn_conv_b': (0.0, 0.1),
     'L0_attn_Dskip': (1.0, 0.6),
     'L0_ffn_b1': (0.0, 0.325),
     'L0_ffn_b2': (0.0, 0.1)}
    factors = {'L0_attn_conv_w': 3.041,
     'L0_attn_W_xproj': 8.0,
     'L0_attn_W_dt': 8.0,
     'L0_attn_b_dt': 21.47,
     'L0_attn_A_log': 38.085}
    for name, (base, spread) in spreads.items():
        noise = np.random.default_rng([zlib.crc32(name.encode()), seed]).standard_normal(out[name].shape)
        drawn = base * np.exp(spread * noise) if base else spread * noise
        out[name] = jnp.asarray(drawn.astype(out[name].dtype))
    for name, factor in factors.items():
        out[name] = (out[name] * factor).astype(out[name].dtype)
    return out
```

```python
from contextlib import ExitStack

import concourse.bass as bass
from concourse import mybir

ALU = mybir.AluOpType
ACT = mybir.ActivationFunctionType
F32 = mybir.dt.float32
I32 = mybir.dt.int32
U32 = mybir.dt.uint32
AX_X = mybir.AxisListType.X


class Chain:

    def __init__(self, eng, sem):
        self.eng, self.sem, self.base, self.local = eng, sem, 0, 0

    def then(self, ins):
        ins.then_inc(self.sem, 1)
        self.local += 1

    def settle(self):
        self.eng.wait_ge(self.sem, self.base + self.local)

    def enter(self, turn, per_turn):
        self.start, self.per_turn = self.base + self.local, per_turn
        self.base, self.local = self.start + turn * per_turn, 0

    def leave(self, turns):
        assert self.local == self.per_turn, (self.local, self.per_turn)
        self.base, self.local = self.start + turns * self.per_turn, 0


def tower_kernel(nc, ids, emb_w, ln_w, ln_b, w_in, conv_w, conv_b, w_xp, w_dt, b_dt, a_log, d_skip,
                 w_out, w_router, w1, b1, w2, b2, out):
    P = 128
    VOCAB, C = emb_w.shape
    L, SEQS = ids.shape
    DI = w_out.shape[0]
    NS = a_log.shape[1]
    R = w_dt.shape[0]
    PR = w_xp.shape[1]
    TAPS = conv_w.shape[1]
    E, _, H = w1.shape
    KC, ND, KH = C // P, DI // P, H // P
    GT = 4
    NG = SEQS // GT
    GW = GT * L
    TOPK = 2
    TILES = (TOPK * SEQS * L + E * (P - 1)) // P
    HB = H // 512
    EPS = 1e-5
    A_LOG_MAX = 84.0
    CSL = 4
    ABK = 2
    FB = 4
    assert L == P and PR == R + 2 * NS and TILES % 2 == 1 and ND == CSL == GT

    c_dram = nc.dram_tensor("c_rows", [NG * NS, GW], F32).ap()
    xs_dram = nc.dram_tensor("sorted_in", [TILES * P, C], F32).ap()
    ys_dram = nc.dram_tensor("sorted_out", [TILES * P, C], F32).ap()

    ctx = ExitStack()
    with ctx:
        def sb(name, shape, dt=F32):
            return ctx.enter_context(nc.sbuf_tensor(name, shape, dt))

        def sem(name):
            return ctx.enter_context(nc.semaphore(name))

        ident = sb("ident", [P, P])
        before = sb("before", [P, P])
        ones = sb("ones", [P, P])
        iota_e = sb("iota_e", [P, E])
        iota_k = sb("iota_k", [P, SEQS])
        iota_t = sb("iota_t", [P, TILES])
        h_res = sb("h_res", [P, SEQS, C])
        st1 = sb("st1", [P, SEQS, 6])
        mv1 = sb("mv1", [P, SEQS, 2])
        mv2 = sb("mv2", [P, SEQS, 2])
        mv3 = sb("mv3", [P, SEQS, 2])
        std = sb("std", [P, SEQS])
        rstd1 = sb("rstd1", [P, SEQS])
        rstd2 = sb("rstd2", [P, SEQS])
        rstd3 = sb("rstd3", [P, SEQS])
        id_raw = sb("id_raw", [P, SEQS], I32)
        id_f = sb("id_f", [P, SEQS])
        id_c = sb("id_c", [P, SEQS])
        id_ok = sb("id_ok", [P, SEQS])
        id_u = sb("id_u", [P, SEQS], U32)
        gate = sb("gate", [P, TOPK, SEQS])
        slot_u = sb("slot_u", [P, TOPK, SEQS], U32)
        tile_e = sb("tile_e", [P, TILES], I32)
        router_sb = sb("router_sb", [P, KC, E])
        xt = sb("xt", [P, 2, C])
        xT = sb("xT", [P, 2, KC * P])
        hact = sb("hact", [P, 2, H])
        hT = sb("hT", [P, KH * P])
        yt = sb("yt", [P, 2, C])
        idx8 = sb("idx8", [P, SEQS, 8], U32)
        zero_row = sb("zero_row", [P, C])

        WORDS = 168 * 256
        arena = sb("arena", [P, WORDS])
        at = [0]

        def carve(*shape):
            size = 1
            for n in shape:
                size *= n
            v = arena[:, at[0]:at[0] + size]
            at[0] += size
            assert at[0] <= WORDS, at
            if len(shape) == 2:
                v = v.rearrange("p (a b) -> p a b", b=shape[1])
            elif len(shape) == 3:
                v = v.rearrange("p (a b c) -> p a b c", b=shape[1], c=shape[2])
            return v

        xconv = carve(NG, ND, GW)
        zgate = carve(NG, ND, GW)
        dt_sb = carve(NG, ND, GW)
        projT = carve(NG, GW)
        wxp_sb = carve(ND, PR)
        wdt_sb = carve(DI)
        wout_sb = carve(ND, C)
        lnw_sb = carve(KC)
        lnb_sb = carve(KC)
        convw_sb = carve(ND, TAPS)
        convb_sb = carve(ND)
        bdt_sb = carve(ND)
        a_sb = carve(ND, NS)
        dskip_sb = carve(ND)
        dtu = carve(ND, GW)
        x1tmp = carve(2, C)
        front_at = at[0]
        win_sb = carve(KC, 2 * DI)
        xn4 = carve(GT, C)
        xnT = carve(KC, GW)
        conv_acc = carve(2, GW)
        sp_e = carve(2, GW)
        sp_t = carve(2, GW)
        sp_r = carve(2, GW)
        at[0] = front_at
        h_buf = carve(ND, GW)
        dbu = carve(ND, GW)
        g_buf = carve(ND, GW)
        c_bc = carve(CSL, GW)
        yg = carve(ND, GW)
        at[0] = 0
        w1_sb = carve(E, KC, H)
        w2_sb = carve(E, KH, C)
        b1_bc = carve(E, H)
        b2_bc = carve(E, C)
        W2_EARLY = E // 2
        at[0] = E * KC * H + W2_EARLY * KH * C
        x2 = carve(SEQS, C)
        x2T = carve(2, KC * P)
        lg = carve(SEQS, E)
        top8 = carve(SEQS, 8)
        ex = carve(SEQS, E)
        ssum = carve(SEQS)
        rsum = carve(SEQS)
        pk = carve(TOPK, SEQS)
        pden = carve(SEQS)
        idx_f = carve(TOPK, SEQS)
        oh = carve(TOPK, SEQS, E)
        hot = carve(SEQS, E)
        cnt_et = carve(E, SEQS)
        inc_et = carve(E, SEQS)
        seg = carve(E, SEQS)
        place = carve(SEQS, E)
        cmp_k = carve(E, SEQS)
        nt_e = carve(E)
        cum_e = carve(E)
        off_e = carve(E)
        cmp_t = carve(TILES, E)
        tile_f = carve(TILES)
        slot_f = carve(TOPK, SEQS)
        picked = carve(TOPK, SEQS, E)
        at[0] = 0
        rows = carve(TOPK, SEQS, C)

        psum = [ctx.enter_context(nc.psum_tensor(f"bank{b}", [P, 512], F32)) for b in range(8)]
        y_ps, a_ps, b_ps, o_ps = psum[0:ND], psum[4:4 + ABK], psum[6], psum[7]

        ids_in, weights_in, setup_done = sem("ids_in"), sem("weights_in"), sem("setup_done")
        emb_in = [sem(f"emb_in{g}") for g in range(NG)]
        ids_clean, var_ready, std_ready, a_exp, a_ready_neg = (
            sem("ids_clean"), sem("var_ready"), sem("std_ready"), sem("a_exp"), sem("a_neg"))
        xn_ready, xnT_ready, front_ready = sem("xn_ready"), sem("xnT_ready"), sem("front_ready")
        conv_started, conv_done, xconv_ready, zgate_ready = (
            sem("conv_started"), sem("conv_done"), sem("xconv_ready"), sem("zgate_ready"))
        proj_ready, c_stored, step_read, step_logged, dt_ready = (
            sem("proj_ready"), sem("c_stored"), sem("step_read"), sem("step_logged"), sem("dt_ready"))
        c_in = [sem(f"c_in{k}") for k in range(CSL)]
        decay_ready, b_ready, dbu_ready, scan_ready, g_ready, g_used = (
            sem("decay_ready"), sem("b_ready"), sem("dbu_ready"), sem("scan_ready"), sem("g_ready"), sem("g_used"))
        y_ready, yg_ready, mix_ready, h2_ready = sem("y_ready"), sem("yg_ready"), sem("mix_ready"), sem("h2_ready")
        x2_ready, x2_turned, x2T_ready, logits_ready = (
            sem("x2_ready"), sem("x2_turned"), sem("x2T_ready"), sem("logits_ready"))
        shifted, expo_ready, hot_ready, ranks_ready, slots_ready, lists_ready = (
            sem("shifted"), sem("expo_ready"), sem("hot_ready"), sem("ranks_ready"), sem("slots_ready"),
            sem("lists_ready"))
        zero_stored, scattered, mixer_done = sem("zero_stored"), sem("scattered"), sem("mixer_done")
        b_in, experts_ready = sem("bias_in"), sem("experts_ready")
        e_in = [sem(f"expert_in{e}") for e in range(E)]
        x_in = [sem(f"xt_in{k}") for k in range(2)]
        y_out, yt_free = sem("yt_stored"), sem("yt_free")
        xt_turned, xT_ready, up_ready, biased, hact_ready, hid_turned, hT0_ready, hT1_ready, down_ready, yt_ready = (
            sem("xt_turned"), sem("xT_ready"), sem("up_ready"), sem("biased"), sem("hact_ready"), sem("hid_turned"),
            sem("hT0_ready"), sem("hT1_ready"), sem("down_ready"), sem("yt_ready"))
        rows_in = [sem(f"rows_in{g}") for g in range(NG)]
        final_ready, out_stored = sem("final_ready"), sem("out_stored")
        dtu_ready, rows_clear, pool_turns, a_bounded = sem("dtu_ready"), sem("rows_clear"), sem("pool_turns"), sem("a_bounded")
        dve_chain, act_chain, pool_chain = sem("dve_chain"), sem("act_chain"), sem("pool_chain")

        def bc(ap, axis, *shape):
            return ap.unsqueeze(axis).broadcast_to([P, *shape])

        def seqs(ap):
            return ap.rearrange("p (s t) -> p s t", t=L)

        FRONT = KC + 2 * ND + 1 + ND
        T_AT, X_AT, Z_AT, P_AT, D_AT = 0, KC, KC + ND, KC + 2 * ND, KC + 2 * ND + 1

        def fbank(k):
            return psum[k % FB]

        block = ctx.enter_context(nc.Block())

        @block.sync
        def _(sp):
            sp.dma_start(id_raw[:, :], ids).then_inc(ids_in, 16)
            loads = [
                (lnw_sb, ln_w.rearrange("(k p) -> p k", p=P)), (lnb_sb, ln_b.rearrange("(k p) -> p k", p=P)),
                (win_sb, w_in.rearrange("(k p) e -> p k e", p=P)),
                (convw_sb, conv_w.rearrange("(k p) t -> p k t", p=P)),
                (convb_sb, conv_b.rearrange("(k p) -> p k", p=P)),
                (wxp_sb, w_xp.rearrange("(k p) e -> p k e", p=P)), (wdt_sb[0:R, :], w_dt),
                (bdt_sb, b_dt.rearrange("(k p) -> p k", p=P)),
                (a_sb, a_log.rearrange("(k p) n -> p k n", p=P)),
                (dskip_sb, d_skip.rearrange("(k p) -> p k", p=P)),
                (wout_sb, w_out.rearrange("(k p) c -> p k c", p=P)),
                (router_sb[:, :, :], w_router.rearrange("(k p) e -> p k e", p=P)),
            ]
            assert len(loads) == 12
            for dst, src in loads:
                sp.dma_start(dst, src, allow_slow_non_contiguous=True).then_inc(weights_in, 16)
            sp.wait_ge(setup_done, 1)
            with sp.Fori(0, TILES) as i:
                sp.dma_start(xs_dram[bass.ts(i, P), :], zero_row[:, :]).then_inc(zero_stored, 16)
            with sp.Fori(0, NG) as g:
                sp.wait_ge(proj_ready, g + 1)
                sp.dma_start(c_dram[bass.ts(g, NS), :], projT[R + NS:PR, g, :]).then_inc(c_stored, 16)
            sp.wait_ge(c_stored, 16 * NG)
            sp.wait_ge(dt_ready, 1 + ND * NG)

            def load_c(q, k):
                sp.dma_start(c_bc[:, k, :], c_dram[bass.ds(q, 1), :].broadcast_to([P, GW])).then_inc(c_in[k], 16)

            for k in range(CSL):
                load_c(k, k)
            with sp.Fori(1, NG * NS // CSL) as m:
                for k in range(CSL):
                    q = m * CSL + k
                    sp.wait_ge(g_ready, ND + ND * (q - CSL + 1))
                    load_c(q, k)

            sp.wait_ge(mixer_done, 1)
            sp.dma_start(b1_bc.rearrange("p e h -> p (e h)"),
                         b1.rearrange("(a e) h -> a (e h)", a=1).broadcast_to([P, E * H])).then_inc(b_in, 16)
            sp.dma_start(b2_bc.rearrange("p e c -> p (e c)"),
                         b2.rearrange("(a e) c -> a (e c)", a=1).broadcast_to([P, E * C])).then_inc(b_in, 16)
            for e in range(E):
                sp.dma_start(w1_sb[:, e, :, :], w1[e].rearrange("(k p) h -> p k h", p=P)).then_inc(e_in[e], 16)
                if e < W2_EARLY:
                    sp.dma_start(w2_sb[:, e, :, :], w2[e].rearrange("(k p) c -> p k c", p=P)).then_inc(e_in[e], 16)
            sp.wait_ge(lists_ready, 1)
            sp.wait_ge(scattered, 16 * TOPK * SEQS)

            def load_x(i, k):
                sp.dma_start(xt[:, k, :], xs_dram[bass.ts(i, P), :]).then_inc(x_in[k], 16)

            load_x(0, 0)
            load_x(1, 1)
            for e in range(W2_EARLY, E):
                sp.dma_start(w2_sb[:, e, :, :], w2[e].rearrange("(k p) c -> p k c", p=P)).then_inc(e_in[e], 16)
            sp.wait_ge(b_in, 32)
            for e in range(E):
                sp.wait_ge(e_in[e], 32)
                sp.sem_inc(experts_ready, 1)
            with sp.Fori(0, TILES // 2 - 1) as m:
                for k in range(2):
                    i = 2 * m + 2 + k
                    sp.wait_ge(xt_turned, i - 1)
                    load_x(i, k)
            sp.wait_ge(xt_turned, TILES - 2)
            load_x(TILES - 1, 0)

        @block.gpsimd
        def _(pool):
            chain = Chain(pool, pool_chain)
            pool.sem_inc(dt_ready, 1)
            pool.sem_inc(yt_free, 2)
            nc.gpsimd.memset(zero_row[:, :], 0.0).then_inc(setup_done, 1)
            chain.then(nc.gpsimd.memset(ident[:, :], 0.0))
            chain.then(nc.gpsimd.memset(before[:, :], 1.0))
            chain.then(nc.gpsimd.memset(ones[:, :], 1.0))
            chain.then(nc.gpsimd.iota(iota_e[:, :], [[1, E]], 0, 0, allow_small_or_imprecise_dtypes=True))
            chain.then(nc.gpsimd.iota(iota_k[:, :], [[P, SEQS]], 0, 0, allow_small_or_imprecise_dtypes=True))
            chain.then(nc.gpsimd.iota(iota_t[:, :], [[1, TILES]], 0, 0, allow_small_or_imprecise_dtypes=True))
            chain.settle()
            nc.gpsimd.affine_select(out=ident[:, :], in_=ident[:, :], compare_op=ALU.not_equal, fill=1.0,
                                    base=0, pattern=[[-1, P]], channel_multiplier=1).then_inc(setup_done, 1)
            nc.gpsimd.affine_select(out=before[:, :], in_=before[:, :], compare_op=ALU.is_gt, fill=0.0,
                                    base=0, pattern=[[1, P]], channel_multiplier=-1).then_inc(setup_done, 1)
            pool.wait_ge(ids_clean, 1)
            for i in range(SEQS):
                nc.gpsimd.indirect_dma_start(
                    out=h_res[:, i, :], out_offset=None, in_=emb_w,
                    in_offset=bass.IndirectOffsetOnAxis(ap=id_u[:, i:i + 1], axis=0)).then_inc(emb_in[i // GT], 16)
            with pool.Fori(0, NG) as g:
                chain.enter(g, 3 * ND)

                def past():
                    pool.sem_inc(pool_turns, 1)

                for d in range(ND):
                    k = d % 2
                    pool.wait_ge(step_logged, g * ND + d + 1)
                    past()
                    chain.then(nc.gpsimd.tensor_scalar(sp_t[:, k, :], sp_e[:, k, :], 1.0, -1.0, ALU.add, ALU.add))
                    chain.settle()
                    past()
                    chain.then(nc.gpsimd.tensor_tensor(sp_t[:, k, :], sp_e[:, k, :], sp_t[:, k, :], ALU.subtract))
                    chain.settle()
                    past()
                    chain.then(nc.gpsimd.tensor_tensor(sp_t[:, k, :], sp_t[:, k, :], dt_sb[:, g, d, :], ALU.add))
                    chain.settle()
                    past()
                    nc.gpsimd.tensor_tensor(dt_sb[:, g, d, :], sp_t[:, k, :], sp_r[:, k, :],
                                            ALU.add).then_inc(dt_ready, 1)
                chain.leave(NG)
            pool.sem_inc(g_ready, ND)
            with pool.Fori(0, NG * NS // CSL) as m:
                for k in range(CSL):
                    for d in range(ND):
                        u = (m * CSL + k) * ND + d
                        if d == 0:
                            pool.wait_ge(c_in[k], 16 * m + 16)
                        pool.wait_ge(scan_ready, ABK + u + 1)
                        pool.wait_ge(g_used, u + 1)
                        nc.gpsimd.tensor_tensor(g_buf[:, d, :], h_buf[:, d, :], c_bc[:, k, :],
                                                ALU.mult).then_inc(g_ready, 1)
            pool.wait_ge(zero_stored, 16 * TILES)
            pool.wait_ge(slots_ready, 1)
            for j in range(TOPK):
                for i in range(SEQS):
                    nc.gpsimd.indirect_dma_start(
                        out=xs_dram, out_offset=bass.IndirectOffsetOnAxis(ap=slot_u[:, j, i:i + 1], axis=0),
                        in_=x2[:, i, :], in_offset=None).then_inc(scattered, 16)

            def store(i, k):
                pool.wait_ge(yt_ready, 1 + i + 1)
                pool.dma_start(ys_dram[bass.ts(i, P), :], yt[:, k, :]).then_inc(y_out, 16)
                pool.wait_ge(y_out, 16 * i + 16)
                pool.sem_inc(yt_free, 1)

            with pool.Fori(0, TILES // 2) as m:
                store(2 * m, 0)
                store(2 * m + 1, 1)
            store(TILES - 1, 0)
            for i in range(SEQS):
                for j in range(TOPK):
                    nc.gpsimd.indirect_dma_start(
                        out=rows[:, j, i, :], out_offset=None, in_=ys_dram,
                        in_offset=bass.IndirectOffsetOnAxis(ap=slot_u[:, j, i:i + 1], axis=0)
                    ).then_inc(rows_in[i // GT], 16)
            for i in range(SEQS):
                pool.wait_ge(final_ready, i + 1)
                pool.dma_start(out[i], h_res[:, i, :]).then_inc(out_stored, 16)
            pool.wait_ge(out_stored, 16 * SEQS)

        @block.scalar
        def _(act):
            chain = Chain(act, act_chain)
            for started in (xconv_ready, step_read, xT_ready, hT0_ready):
                act.sem_inc(started, 1)
            for r in range(2):
                act.wait_ge(var_ready, r + 1)
                nc.scalar.activation(std[:, :], std[:, :], ACT.Sqrt).then_inc(std_ready, 1)
            act.wait_ge(weights_in, 16 * 12)
            act.wait_ge(a_bounded, 1)
            nc.scalar.activation(a_sb, a_sb, ACT.Exp).then_inc(a_exp, 1)

            act.wait_ge(rows_clear, 1)
            with act.Fori(0, NG) as g:
                chain.enter(g, 2 * ND)
                for c in range(KC):
                    act.wait_ge(front_ready, g * FRONT + T_AT + c + 1)
                    nc.scalar.activation(xnT[:, c, :], fbank(T_AT + c)[:, :], ACT.Identity,
                                         bias=lnb_sb[:, c:c + 1], scale=lnw_sb[:, c:c + 1]).then_inc(xnT_ready, 1)

                def conv_start(d):
                    act.wait_ge(xconv_ready, 1 + g * ND + max(d - 1, 0))
                    act.wait_ge(front_ready, g * FRONT + X_AT + d + 1)
                    nc.scalar.activation(conv_acc[:, d % 2, :], fbank(X_AT + d)[:, :], ACT.Identity,
                                         bias=convb_sb[:, d:d + 1],
                                         scale=convw_sb[:, d, TAPS - 1:TAPS]).then_inc(conv_started, 1)

                def conv_end(d):
                    act.wait_ge(conv_done, g * ND + d + 1)
                    nc.scalar.activation(xconv[:, g, d, :], conv_acc[:, d % 2, :], ACT.Silu).then_inc(xconv_ready, 1)

                conv_start(0)
                for d in range(1, ND):
                    conv_start(d)
                    conv_end(d - 1)
                conv_end(ND - 1)
                for d in range(ND):
                    act.wait_ge(front_ready, g * FRONT + Z_AT + d + 1)
                    nc.scalar.activation(zgate[:, g, d, :], fbank(Z_AT + d)[:, :], ACT.Silu).then_inc(zgate_ready, 1)
                act.wait_ge(front_ready, g * FRONT + P_AT + 1)
                nc.scalar.activation(projT[0:PR, g, :], fbank(P_AT)[0:PR, :], ACT.Copy).then_inc(proj_ready, 1)
                for d in range(ND):
                    k = d % 2
                    bank = fbank(D_AT + d)
                    act.wait_ge(front_ready, g * FRONT + D_AT + d + 1)
                    act.wait_ge(dt_ready, 1 + g * ND + max(d - 1, 0))
                    chain.then(nc.scalar.activation(sp_e[:, k, :], bank[:, :], ACT.Abs, bias=bdt_sb[:, d:d + 1]))
                    nc.scalar.activation(sp_r[:, k, :], bank[:, :], ACT.Relu,
                                         bias=bdt_sb[:, d:d + 1]).then_inc(step_read, 1)
                    chain.settle()
                    chain.then(nc.scalar.activation(sp_e[:, k, :], sp_e[:, k, :], ACT.Exp, scale=-1.0))
                    chain.settle()
                    nc.scalar.activation(dt_sb[:, g, d, :], sp_e[:, k, :], ACT.Ln, bias=1.0).then_inc(step_logged, 1)
                chain.leave(NG)

            act.wait_ge(a_ready_neg, 1)
            act.wait_ge(dt_ready, 1 + ND * NG)
            with act.Fori(0, NG) as g:
                with act.Fori(0, NS) as n:
                    for d in range(ND):
                        u = (g * NS + n) * ND + d
                        act.wait_ge(scan_ready, u + 1)
                        nc.scalar.activation(seqs(a_ps[d % ABK][:, :])[:, :, 1:L], seqs(dt_sb[:, g, d, :])[:, :, 1:L],
                                             ACT.Exp, scale=a_sb[:, d, bass.ds(n, 1)]).then_inc(decay_ready, 1)

            act.wait_ge(var_ready, 3)
            nc.scalar.activation(std[:, :], std[:, :], ACT.Sqrt).then_inc(std_ready, 1)
            for i in range(SEQS):
                act.wait_ge(x2_turned, i + 1)
                nc.scalar.activation(x2T[:, i % 2, :], psum[i % 2][:, 0:KC * P], ACT.Copy).then_inc(x2T_ready, 1)
            act.wait_ge(shifted, 1)
            nc.scalar.activation(ex, ex, ACT.Exp).then_inc(expo_ready, 1)

            def up(i, k):
                act.wait_ge(xt_turned, i + 1)
                nc.scalar.activation(xT[:, k, :], psum[6][:, 0:KC * P], ACT.Copy).then_inc(xT_ready, 1)
                for b in range(HB):
                    act.wait_ge(biased, HB * i + b + 1)
                    nc.scalar.activation(hact[:, k, bass.ts(b, 512)], psum[2 * k + b][:, :],
                                         ACT.Gelu_apprx_tanh).then_inc(hact_ready, 1)

            def down(i, k):
                act.wait_ge(hid_turned, 2 * i + 1)
                nc.scalar.activation(hT[:, 0:512], psum[4][:, :], ACT.Copy).then_inc(hT0_ready, 1)

            up(0, 0)
            with act.Fori(0, TILES // 2) as m:
                for k in range(2):
                    up(2 * m + k + 1, 1 - k)
                    down(2 * m + k, k)
            down(TILES - 1, 0)

        @block.vector
        def _(dve):
            chain = Chain(dve, dve_chain)
            for started in (dbu_ready, yg_ready, hT1_ready, yt_ready):
                dve.sem_inc(started, 1)
            dve.wait_ge(ids_in, 16)
            chain.then(nc.vector.tensor_copy(id_f[:, :], id_raw[:, :]))
            chain.settle()
            chain.then(nc.vector.tensor_scalar(id_c[:, :], id_f[:, :], 0.0, float(VOCAB - 1), ALU.max, ALU.min))
            chain.settle()
            nc.vector.tensor_copy(id_u[:, :], id_c[:, :]).then_inc(ids_clean, 1)
            chain.then(nc.vector.tensor_tensor(id_ok[:, :], id_c[:, :], id_f[:, :], ALU.is_equal))
            chain.settle()
            nc.vector.memset(projT, 0.0).then_inc(rows_clear, 1)
            for i in range(SEQS):
                if i % GT == 0:
                    dve.wait_ge(emb_in[i // GT], 16 * GT)
                chain.then(nc.vector.tensor_scalar(h_res[:, i, :], h_res[:, i, :], id_ok[:, i:i + 1], None, ALU.mult))
                chain.settle()
                chain.then(nc.vector.bn_stats(st1[:, i, :], h_res[:, i, :]))
            chain.settle()

            def reciprocal_root(mv, rstd, turn):
                for i in range(SEQS):
                    chain.then(nc.vector.bn_aggr(mv[:, i, :], st1[:, i, :]))
                chain.settle()
                nc.vector.tensor_scalar(std[:, :], mv[:, :, 1], EPS, None, ALU.add).then_inc(var_ready, 1)
                dve.wait_ge(std_ready, turn)
                chain.then(nc.vector.reciprocal(rstd[:, :], std[:, :]))
                chain.settle()

            reciprocal_root(mv1, rstd1, 1)
            with dve.Fori(0, SEQS // 2) as m:
                chain.enter(m, 4)
                for k in range(2):
                    i = 2 * m + k
                    chain.then(nc.vector.tensor_scalar(x1tmp[:, k, :], h_res[:, i, :], mv1[:, i, 0:1],
                                                       rstd1[:, bass.ds(i, 1)], ALU.subtract, ALU.mult))
                    chain.settle()
                    chain.then(nc.vector.bn_stats(st1[:, i, :], x1tmp[:, k, :]))
                chain.leave(SEQS // 2)
            chain.settle()
            reciprocal_root(mv2, rstd2, 2)
            dve.wait_ge(weights_in, 16 * 12)
            nc.vector.tensor_scalar(a_sb, a_sb, A_LOG_MAX, None, ALU.min).then_inc(a_bounded, 1)
            dve.wait_ge(a_exp, 1)
            nc.vector.tensor_scalar(a_sb, a_sb, -1.0, None, ALU.mult).then_inc(a_ready_neg, 1)
            dve.wait_ge(weights_in, 16 * 12)

            with dve.Fori(0, NG) as g:
                chain.enter(g, GT + (TAPS - 2) * ND)
                for j in range(GT):
                    i = g * GT + j
                    chain.then(nc.vector.tensor_scalar(xn4[:, j, :], h_res[:, i, :], mv1[:, i, 0:1],
                                                       rstd1[:, bass.ds(i, 1)], ALU.subtract, ALU.mult))
                    chain.settle()
                    nc.vector.tensor_scalar(xn4[:, j, :], xn4[:, j, :], mv2[:, i, 0:1], rstd2[:, bass.ds(i, 1)],
                                            ALU.subtract, ALU.mult).then_inc(xn_ready, 1)
                for d in range(ND):
                    dve.wait_ge(conv_started, g * ND + d + 1)
                    x_in_ps, acc = seqs(fbank(X_AT + d)[:, :]), seqs(conv_acc[:, d % 2, :])
                    for back in range(1, TAPS):
                        ins = nc.vector.scalar_tensor_tensor(
                            out=acc[:, :, back:L], in0=x_in_ps[:, :, 0:L - back],
                            scalar=convw_sb[:, d, TAPS - 1 - back:TAPS - back], in1=acc[:, :, back:L],
                            op0=ALU.mult, op1=ALU.add)
                        if back < TAPS - 1:
                            chain.then(ins)
                            chain.settle()
                        else:
                            ins.then_inc(conv_done, 1)
                chain.leave(NG)

            dve.wait_ge(dt_ready, 1 + ND * NG)
            for k in range(ABK):
                nc.vector.memset(seqs(a_ps[k][:, :])[:, :, 0:1], 0.0).then_inc(scan_ready, 1)
            with dve.Fori(0, NG) as g:
                chain.enter(g, ND + 2 * GT + GT)
                for d in range(ND):
                    nc.vector.tensor_tensor(dtu[:, d, :], dt_sb[:, g, d, :], xconv[:, g, d, :],
                                            ALU.mult).then_inc(dtu_ready, 1)
                with dve.Fori(0, NS) as n:
                    q = g * NS + n

                    def input_of(d):
                        if d == 0:
                            dve.wait_ge(dtu_ready, g * ND + ND)
                            dve.wait_ge(b_ready, q + 1)
                        nc.vector.tensor_tensor(dbu[:, d, :], dtu[:, d, :], b_ps[:, :],
                                                ALU.mult).then_inc(dbu_ready, 1)

                    def scan_of(d):
                        u = q * ND + d
                        dve.wait_ge(decay_ready, u + 1)
                        dve.wait_ge(dbu_ready, 1 + u + 1)
                        dve.wait_ge(g_ready, u + 1)
                        nc.vector.tensor_tensor_scan(h_buf[:, d, :], a_ps[d % ABK][:, :], dbu[:, d, :], 0.0,
                                                     ALU.mult, ALU.add).then_inc(scan_ready, 1)

                    input_of(0)
                    for d in range(1, ND):
                        input_of(d)
                        scan_of(d - 1)
                    scan_of(ND - 1)
                for d in range(ND):
                    dve.wait_ge(y_ready, g * ND + d + 1)
                    chain.then(nc.vector.scalar_tensor_tensor(
                        out=yg[:, d, :], in0=xconv[:, g, d, :], scalar=dskip_sb[:, d:d + 1], in1=y_ps[d][:, :],
                        op0=ALU.mult, op1=ALU.add))
                    chain.settle()
                    nc.vector.tensor_tensor(yg[:, d, :], yg[:, d, :], zgate[:, g, d, :],
                                            ALU.mult).then_inc(yg_ready, 1)
                for j in range(GT):
                    i = g * GT + j
                    chain.then(nc.vector.tensor_scalar(x1tmp[:, j % 2, :], h_res[:, i, :], mv1[:, i, 0:1],
                                                       rstd1[:, bass.ds(i, 1)], ALU.subtract, ALU.mult))
                    chain.settle()
                    chain.then(nc.vector.tensor_tensor(h_res[:, i, :], h_res[:, i, :], x1tmp[:, j % 2, :], ALU.add))
                    dve.wait_ge(mix_ready, 2 * g + j // 2 + 1)
                    chain.settle()
                    nc.vector.tensor_tensor(h_res[:, i, :], h_res[:, i, :], o_ps[:, (j % 2) * C:(j % 2 + 1) * C],
                                            ALU.add).then_inc(h2_ready, 1)
                    dve.wait_ge(h2_ready, i + 1)
                    chain.then(nc.vector.bn_stats(st1[:, i, :], h_res[:, i, :]))
                chain.leave(NG)
            chain.settle()
            dve.sem_inc(mixer_done, 1)
            reciprocal_root(mv3, rstd3, 3)
            for i in range(SEQS):
                nc.vector.tensor_scalar(x2[:, i, :], h_res[:, i, :], mv3[:, i, 0:1], rstd3[:, i:i + 1],
                                        ALU.subtract, ALU.mult).then_inc(x2_ready, 1)

            dve.wait_ge(logits_ready, SEQS)
            chain.then(nc.vector.tensor_copy(lg, psum[2][:, 0:SEQS * E].rearrange("p (i e) -> p i e", e=E)))
            chain.settle()
            for i in range(SEQS):
                chain.then(nc.vector.max(top8[:, i, :], lg[:, i, :]))
            chain.settle()
            nc.vector.tensor_tensor(ex, lg, top8[:, :, 0:1].broadcast_to([P, SEQS, E]),
                                    ALU.subtract).then_inc(shifted, 1)
            for i in range(SEQS):
                chain.then(nc.vector.max_index(idx8[:, i, :], top8[:, i, :], lg[:, i, :]))
            chain.settle()
            for j in range(TOPK):
                chain.then(nc.vector.tensor_copy(idx_f[:, j, :], idx8[:, :, j]))
            chain.settle()
            for j in range(TOPK):
                chain.then(nc.vector.tensor_tensor(oh[:, j, :, :], bc(idx_f[:, j, :], 2, SEQS, E),
                                                   bc(iota_e[:, :], 1, SEQS, E), ALU.is_equal))
            chain.settle()
            nc.vector.tensor_tensor(hot, oh[:, 0, :, :], oh[:, 1, :, :], ALU.add).then_inc(hot_ready, 1)
            dve.wait_ge(expo_ready, 1)
            chain.then(nc.vector.reduce_sum(ssum, ex, AX_X))
            chain.settle()
            chain.then(nc.vector.reciprocal(rsum, ssum))
            for j in range(TOPK):
                chain.then(nc.vector.tensor_tensor(picked[:, j, :, :], oh[:, j, :, :], ex, ALU.mult))
            chain.settle()
            for j in range(TOPK):
                chain.then(nc.vector.reduce_sum(pk[:, j, :], picked[:, j, :, :], AX_X))
            chain.settle()
            for j in range(TOPK):
                chain.then(nc.vector.tensor_tensor(pk[:, j, :], pk[:, j, :], rsum, ALU.mult))
            chain.settle()
            chain.then(nc.vector.tensor_tensor(pden, pk[:, 0, :], pk[:, 1, :], ALU.add))
            chain.settle()
            chain.then(nc.vector.tensor_scalar(pden, pden, 1e-8, None, ALU.add))
            chain.settle()
            chain.then(nc.vector.reciprocal(pden, pden))
            chain.settle()
            for j in range(TOPK):
                chain.then(nc.vector.tensor_tensor(gate[:, j, :], pk[:, j, :], pden, ALU.mult))

            dve.wait_ge(ranks_ready, 1)
            chain.then(nc.vector.tensor_copy(cnt_et, psum[4][:, 0:SEQS * E].rearrange("p (i e) -> p e i", e=E)))
            chain.then(nc.vector.memset(seg, 1.0))
            chain.settle()
            chain.then(nc.vector.memset(seg[:, :, 0:1], 0.0))
            chain.settle()
            chain.then(nc.vector.tensor_tensor_scan(inc_et.rearrange("p e i -> p (e i)"), seg.rearrange("p e i -> p (e i)"),
                                                    cnt_et.rearrange("p e i -> p (e i)"), 0.0, ALU.mult, ALU.add))
            chain.settle()
            chain.then(nc.vector.tensor_tensor(cmp_k, inc_et[:, :, SEQS - 1:SEQS].broadcast_to([P, E, SEQS]),
                                               bc(iota_k[:, :], 1, E, SEQS), ALU.is_gt))
            chain.settle()
            chain.then(nc.vector.reduce_sum(nt_e, cmp_k, AX_X))
            chain.settle()
            chain.then(nc.vector.tensor_tensor_scan(cum_e, ones[:, 0:E], nt_e, 0.0, ALU.mult, ALU.add))
            chain.settle()
            chain.then(nc.vector.tensor_tensor(off_e, cum_e, nt_e, ALU.subtract))
            chain.then(nc.vector.tensor_tensor(cmp_t, bc(cum_e, 1, TILES, E), bc(iota_t[:, :], 2, TILES, E), ALU.is_le))
            chain.settle()
            chain.then(nc.vector.tensor_scalar(off_e, off_e, float(P), None, ALU.mult))
            chain.then(nc.vector.reduce_sum(tile_f, cmp_t, AX_X))
            chain.settle()
            chain.then(nc.vector.tensor_scalar(tile_e[:, :], tile_f, float(E - 1), None, ALU.min))
            chain.then(nc.vector.tensor_tensor(inc_et, inc_et, cnt_et, ALU.subtract))
            chain.settle()
            chain.then(nc.vector.tensor_tensor(inc_et, inc_et, bc(off_e, 2, E, SEQS), ALU.add))
            chain.settle()
            chain.then(nc.vector.tensor_tensor(place, psum[3][:, 0:SEQS * E].rearrange("p (i e) -> p i e", e=E),
                                               inc_et.rearrange("p e i -> p i e"), ALU.add))
            chain.settle()
            for j in range(TOPK):
                chain.then(nc.vector.tensor_tensor(picked[:, j, :, :], oh[:, j, :, :], place, ALU.mult))
            chain.settle()
            for j in range(TOPK):
                chain.then(nc.vector.reduce_sum(slot_f[:, j, :], picked[:, j, :, :], AX_X))
            chain.settle()
            nc.vector.tensor_copy(slot_u[:, :, :], slot_f).then_inc(slots_ready, 1)
            chain.settle()
            dve.sem_inc(lists_ready, 1)

            def up(i, k):
                e = dve.value_load(tile_e[0:1, bass.ds(i, 1)], min_val=0, max_val=E - 1)
                for b in range(HB):
                    dve.wait_ge(up_ready, HB * i + b + 1)
                    nc.vector.tensor_tensor(psum[2 * k + b][:, :], psum[2 * k + b][:, :],
                                            b1_bc[:, bass.ds(e, 1), bass.ts(b, 512)], ALU.add).then_inc(biased, 1)

            def down(i, k):
                e = dve.value_load(tile_e[0:1, bass.ds(i, 1)], min_val=0, max_val=E - 1)
                dve.wait_ge(hid_turned, 2 * i + 2)
                nc.vector.tensor_copy(hT[:, 512:1024], psum[5][:, :]).then_inc(hT1_ready, 1)
                dve.wait_ge(down_ready, i + 1)
                dve.wait_ge(yt_free, i + 1)
                nc.vector.tensor_tensor(yt[:, k, :], psum[7][:, 0:C], b2_bc[:, bass.ds(e, 1), :],
                                        ALU.add).then_inc(yt_ready, 1)

            dve.wait_ge(b_in, 32)
            up(0, 0)
            with dve.Fori(0, TILES // 2) as m:
                for k in range(2):
                    up(2 * m + k + 1, 1 - k)
                    down(2 * m + k, k)
            down(TILES - 1, 0)

            for i in range(SEQS):
                if i % GT == 0:
                    dve.wait_ge(rows_in[i // GT], 16 * TOPK * GT)
                chain.then(nc.vector.scalar_tensor_tensor(
                    out=h_res[:, i, :], in0=rows[:, 0, i, :], scalar=gate[:, 0, i:i + 1], in1=h_res[:, i, :],
                    op0=ALU.mult, op1=ALU.add))
                chain.settle()
                nc.vector.scalar_tensor_tensor(
                    out=h_res[:, i, :], in0=rows[:, 1, i, :], scalar=gate[:, 1, i:i + 1], in1=h_res[:, i, :],
                    op0=ALU.mult, op1=ALU.add).then_inc(final_ready, 1)

        @block.tensor
        def _(pe):
            def mm(dst, lhsT, rhs, first=True, last=True):
                return nc.tensor.matmul(dst, lhsT, rhs, start=first, stop=last)

            pe.wait_ge(setup_done, 3)
            pe.wait_ge(weights_in, 16 * 12)
            with pe.Fori(0, NG) as g:
                pe.wait_ge(step_read, 1 + g * ND)
                pe.wait_ge(xn_ready, g * GT + GT)
                for c in range(KC):
                    for j in range(GT):
                        ins = nc.tensor.transpose(fbank(T_AT + c)[:, bass.ts(j, P)], xn4[:, j, bass.ts(c, P)],
                                                  ident[:, :])
                    ins.then_inc(front_ready, 1)
                pe.wait_ge(xnT_ready, g * KC + KC)
                for d in range(2 * ND):
                    k = X_AT + d
                    last_use = k - FB
                    if last_use >= Z_AT:
                        pe.wait_ge(zgate_ready, g * ND + last_use - Z_AT + 1)
                    elif last_use >= X_AT:
                        pe.wait_ge(conv_done, g * ND + last_use - X_AT + 1)
                    for c in range(KC):
                        ins = mm(fbank(k)[:, :], win_sb[:, c, bass.ts(d, P)], xnT[:, c, :], c == 0, c == KC - 1)
                    ins.then_inc(front_ready, 1)
                pe.wait_ge(xconv_ready, 1 + g * ND + ND)
                pe.wait_ge(zgate_ready, g * ND + P_AT - FB - Z_AT + 1)
                for d in range(ND):
                    ins = mm(fbank(P_AT)[0:PR, :], wxp_sb[:, d, :], xconv[:, g, d, :], d == 0, d == ND - 1)
                ins.then_inc(front_ready, 1)
                pe.wait_ge(zgate_ready, g * ND + ND)
                pe.wait_ge(proj_ready, g + 1)
                for d in range(ND):
                    mm(fbank(D_AT + d)[:, :], wdt_sb[0:R, bass.ts(d, P)], projT[0:R, g, :]).then_inc(front_ready, 1)

            pe.sem_inc(g_used, ND)
            pe.wait_ge(dt_ready, 1 + ND * NG)
            with pe.Fori(0, NG) as g:
                def b_row(n):
                    pe.wait_ge(dbu_ready, 1 + (g * NS + n) * ND)
                    mm(b_ps[:, :], ident[:, R + n:R + n + 1].broadcast_to([P, P]),
                       projT[:, g, :]).then_inc(b_ready, 1)

                def y_add(n):
                    for d in range(ND):
                        if n == 0 and d == 0:
                            pe.wait_ge(yg_ready, 1 + g * ND)
                        pe.wait_ge(g_ready, ND + (g * NS + n) * ND + d + 1)
                        mm(y_ps[d][:, :], ident[:, :], g_buf[:, d, :], n == 0, n == NS - 1).then_inc(g_used, 1)

                b_row(0)
                for n in range(1, NS):
                    b_row(n)
                    y_add(n - 1)
                y_add(NS - 1)
                for d in range(ND):
                    pe.wait_ge(g_used, ND + g * NS * ND + (NS - 1) * ND + d + 1)
                    pe.sem_inc(y_ready, 1)
                pe.wait_ge(yg_ready, 1 + g * ND + ND)
                for j in range(GT):
                    if j == 2:
                        pe.wait_ge(h2_ready, g * GT + j)
                    for d in range(ND):
                        ins = mm(o_ps[:, (j % 2) * C:(j % 2 + 1) * C], yg[:, d, bass.ts(j, P)], wout_sb[:, d, :],
                                 d == 0, d == ND - 1)
                    if j % 2:
                        ins.then_inc(mix_ready, 1)

            for i in range(SEQS):
                pe.wait_ge(x2_ready, i + 1)
                if i >= 2:
                    pe.wait_ge(x2T_ready, i - 1)
                for c in range(KC):
                    ins = nc.tensor.transpose(psum[i % 2][:, bass.ts(c, P)], x2[:, i, bass.ts(c, P)], ident[:, :])
                ins.then_inc(x2_turned, 1)
                pe.wait_ge(x2T_ready, i + 1)
                for c in range(KC):
                    ins = mm(psum[2][:, bass.ts(i, E)], x2T[:, i % 2, bass.ts(c, P)], router_sb[:, c, :],
                             c == 0, c == KC - 1)
                ins.then_inc(logits_ready, 1)
            pe.wait_ge(hot_ready, 1)
            mm(psum[3][:, 0:SEQS * E], before[:, :], hot.rearrange("p i e -> p (i e)"))
            mm(psum[4][:, 0:SEQS * E], ones[:, :], hot.rearrange("p i e -> p (i e)")).then_inc(ranks_ready, 1)
            pe.wait_ge(lists_ready, 1)

            def up(i, k):
                pe.wait_ge(x_in[k], 16 * (half[0] + 1))
                pe.wait_ge(xT_ready, 1 + i)
                for c in range(KC):
                    ins = nc.tensor.transpose(psum[6][:, bass.ts(c, P)], xt[:, k, bass.ts(c, P)], ident[:, :])
                ins.then_inc(xt_turned, 1)
                e = pe.value_load(tile_e[0:1, bass.ds(i, 1)], min_val=0, max_val=E - 1)
                pe.wait_ge(experts_ready, e + 1)
                pe.wait_ge(xT_ready, 1 + i + 1)
                for b in range(HB):
                    for c in range(KC):
                        ins = mm(psum[2 * k + b][:, :], xT[:, k, bass.ts(c, P)],
                                 w1_sb[:, bass.ds(e, 1), c, bass.ts(b, 512)], c == 0, c == KC - 1)
                    ins.then_inc(up_ready, 1)

            def down(i, k):
                e = pe.value_load(tile_e[0:1, bass.ds(i, 1)], min_val=0, max_val=E - 1)
                for b in range(2):
                    pe.wait_ge(hact_ready, HB * i + b + 1)
                    pe.wait_ge((hT0_ready, hT1_ready)[b], 1 + i)
                    for j in range(4):
                        ins = nc.tensor.transpose(psum[4 + b][:, bass.ts(j, P)], hact[:, k, bass.ts(4 * b + j, P)],
                                                  ident[:, :])
                    ins.then_inc(hid_turned, 1)
                pe.wait_ge(yt_ready, 1 + i)
                pe.wait_ge(hT0_ready, 1 + i + 1)
                pe.wait_ge(hT1_ready, 1 + i + 1)
                for h in range(KH):
                    ins = mm(psum[7][:, 0:C], hT[:, bass.ts(h, P)], w2_sb[:, bass.ds(e, 1), h, :], h == 0, h == KH - 1)
                ins.then_inc(down_ready, 1)

            half = [0]
            up(0, 0)
            with pe.Fori(0, TILES // 2) as m:
                half[0] = m
                up(2 * m + 1, 1)
                down(2 * m, 0)
                half[0] = m + 1
                up(2 * m + 2, 0)
                down(2 * m + 1, 1)
            down(TILES - 1, 0)


def kernel(x, L0_tok_embedding, L0_attn_ln_w, L0_attn_ln_b, L0_attn_W_in, L0_attn_conv_w, L0_attn_conv_b,
           L0_attn_W_xproj, L0_attn_W_dt, L0_attn_b_dt, L0_attn_A_log, L0_attn_Dskip, L0_attn_W_out,
           L0_ffn_router_w, L0_ffn_w1, L0_ffn_b1, L0_ffn_w2, L0_ffn_b2):
    import numpy as _np
    import concourse.bacc as _bacc
    from concourse import mybir as _mybir
    from concourse.bass_utils import run_bass_kernel_spmd as _run

    given = {
        "ids": x.T, "embedding": L0_tok_embedding, "ln_w": L0_attn_ln_w, "ln_b": L0_attn_ln_b,
        "w_in": L0_attn_W_in.T, "conv_w": L0_attn_conv_w, "conv_b": L0_attn_conv_b,
        "w_xproj": L0_attn_W_xproj.T, "w_dt": L0_attn_W_dt.T, "b_dt": L0_attn_b_dt, "a_log": L0_attn_A_log,
        "d_skip": L0_attn_Dskip, "w_out": L0_attn_W_out.T, "router": L0_ffn_router_w.T,
        "w1": L0_ffn_w1.transpose(0, 2, 1), "b1": L0_ffn_b1, "w2": L0_ffn_w2.transpose(0, 2, 1), "b2": L0_ffn_b2,
    }
    nc = _bacc.Bacc("TRN2", target_bir_lowering=False, num_devices=1)
    arrays, args = {}, []
    for name, a in given.items():
        a = _np.ascontiguousarray(a)
        arrays[f"in_{name}"] = a
        args.append(nc.dram_tensor(f"in_{name}", a.shape, _mybir.dt.from_np(a.dtype), kind="ExternalInput").ap())
    seqs, length = x.shape
    shape = (seqs, length, L0_tok_embedding.shape[1])
    args.append(nc.dram_tensor("out", shape, _mybir.dt.float32, kind="ExternalOutput").ap())
    tower_kernel(nc, *args)
    r = _run(nc, [arrays], core_ids=[0])
    return r.results[0]["out"]
```

```python
from contextlib import ExitStack

import concourse.bass as bass
from concourse import mybir

ALU = mybir.AluOpType
ACT = mybir.ActivationFunctionType
F32 = mybir.dt.float32
I32 = mybir.dt.int32
U32 = mybir.dt.uint32
AX_X = mybir.AxisListType.X


class Chain:

    def __init__(self, eng, sem):
        self.eng, self.sem, self.base, self.local = eng, sem, 0, 0

    def then(self, ins):
        ins.then_inc(self.sem, 1)
        self.local += 1

    def settle(self):
        self.eng.wait_ge(self.sem, self.base + self.local)

    def enter(self, turn, per_turn):
        self.start, self.per_turn = self.base + self.local, per_turn
        self.base, self.local = self.start + turn * per_turn, 0

    def leave(self, turns):
        assert self.local == self.per_turn, (self.local, self.per_turn)
        self.base, self.local = self.start + turns * self.per_turn, 0


def tower_kernel(nc, ids, emb_w, ln_w, ln_b, w_in, conv_w, conv_b, w_xp, w_dt, b_dt, a_log, d_skip,
                 w_out, w_router, w1, b1, w2, b2, out):
    P = 128
    VOCAB, C = emb_w.shape
    L, SEQS = ids.shape
    NTOK = SEQS * L
    DI = w_out.shape[0]
    NS = a_log.shape[1]
    R = w_dt.shape[0]
    PR = w_xp.shape[1]
    TAPS = conv_w.shape[1]
    E, _, H = w1.shape
    KC, ND, KH = C // P, DI // P, H // P
    GT = 4
    NG = SEQS // GT
    GW = GT * L
    TOPK = 2
    TILES = (TOPK * NTOK + E * (P - 1)) // P
    BANK = 512
    HB = H // BANK
    EPS = 1e-5
    A_LOG_MAX = 84.0
    CSL = 4
    ABK = 2
    FB = 4
    assert L == P and PR == R + 2 * NS and TILES % 2 == 1 and ND == CSL == GT and GW == BANK

    c_dram = nc.dram_tensor("c_rows", [NG * NS, GW], F32).ap()
    x2_dram = nc.dram_tensor("expert_in", [NTOK, C], F32).ap()
    sum_dram = nc.dram_tensor("sums", [NTOK + P, C], F32).ap()

    ctx = ExitStack()
    with ctx:
        def sb(name, shape, dt=F32):
            return ctx.enter_context(nc.sbuf_tensor(name, shape, dt))

        def sem(name):
            return ctx.enter_context(nc.semaphore(name))

        ident = sb("ident", [P, P])
        before = sb("before", [P, P])
        ones = sb("ones", [P, P])
        iota_p = sb("iota_p", [P, P])
        iota_k = sb("iota_k", [P, SEQS])
        iota_t = sb("iota_t", [P, TILES])
        token = sb("token", [P, SEQS])
        spare = sb("spare", [P, 1])
        power = sb("power", [P, SEQS])
        h_res = sb("h_res", [P, SEQS, C])
        st = sb("st", [P, SEQS, 6])
        mv1 = sb("mv1", [P, SEQS, 2])
        mvg = sb("mvg", [P, GT, 2])
        mvh = sb("mvh", [P, GT, 2])
        var1 = sb("var1", [P, SEQS])
        varg = sb("varg", [P, GT])
        varh = sb("varh", [P, GT])
        rstd1 = sb("rstd1", [P, SEQS])
        rstdg = sb("rstdg", [P, GT])
        rstdh = sb("rstdh", [P, GT])
        id_raw = sb("id_raw", [P, SEQS], I32)
        id_f = sb("id_f", [P, SEQS])
        id_c = sb("id_c", [P, SEQS])
        id_ok = sb("id_ok", [P, SEQS])
        id_u = sb("id_u", [P, SEQS], U32)
        lg = sb("lg", [P, SEQS, E])
        gate_t = sb("gate_t", [P, TILES])
        from_t = sb("from_t", [P, TILES])
        to_t = sb("to_t", [P, TILES])
        from_u = [sb(f"from_u{k}", [P, 1], U32) for k in range(2)]
        to_u = [sb(f"to_u{k}", [P, 1], U32) for k in range(2)]
        tile_e = sb("tile_e", [P, TILES], I32)
        router_sb = sb("router_sb", [P, KC, E])
        xt = sb("xt", [P, 2, C])
        xT = sb("xT", [P, KC * P])
        hact = sb("hact", [P, H])
        hT = sb("hT", [P, KH * P])
        yt = sb("yt", [P, 2, C])
        zero_row = sb("zero_row", [P, C])

        WORDS = 168 * 256
        arena = sb("arena", [P, WORDS])
        at = [0]

        def carve(*shape):
            size = 1
            for n in shape:
                size *= n
            v = arena[:, at[0]:at[0] + size]
            at[0] += size
            assert at[0] <= WORDS, at
            if len(shape) == 2:
                v = v.rearrange("p (a b) -> p a b", b=shape[1])
            elif len(shape) == 3:
                v = v.rearrange("p (a b c) -> p a b c", b=shape[1], c=shape[2])
            return v

        xconv = carve(NG, ND, GW)
        zgate = carve(NG, ND, GW)
        dt_sb = carve(NG, ND, GW)
        projT = carve(NG, GW)
        wxp_sb = carve(ND, PR)
        wdt_sb = carve(DI)
        wout_sb = carve(ND, C)
        lnw_sb = carve(KC)
        lnb_sb = carve(KC)
        convw_sb = carve(ND, TAPS)
        convb_sb = carve(ND)
        bdt_sb = carve(ND)
        a_sb = carve(ND, NS)
        dskip_sb = carve(ND)
        dtu = carve(ND, GW)
        x1tmp = carve(2, C)
        x2 = carve(GT, C)
        front_at = at[0]
        win_sb = carve(KC, 2 * DI)
        xn4 = carve(GT, C)
        xnT = carve(KC, GW)
        conv_acc = carve(2, GW)
        sp_e = carve(2, GW)
        sp_t = carve(2, GW)
        sp_r = carve(2, GW)
        at[0] = front_at
        h_buf = carve(ND, GW)
        dbu = carve(ND, GW)
        g_buf = carve(ND, GW)
        c_bc = carve(CSL, GW)
        yg = carve(ND, GW)
        x2T = hact[:, :]
        assert GT * KC * P == H
        at[0] = 0
        w1_sb = carve(E, KC, H)
        w2_sb = carve(E, KH, C)
        b1_bc = carve(E, H)
        b2_bc = carve(E, C)
        W2_EARLY = 2
        at[0] = E * KC * H + W2_EARLY * KH * C
        hot_b = carve(TOPK * SEQS, P)
        to_add = carve(TOPK * SEQS, 3, TILES)
        top8 = carve(SEQS, 8)
        idx8 = carve(SEQS, 8).bitcast(U32)
        ex = carve(SEQS, E)
        ssum = carve(SEQS)
        rsum = carve(SEQS)
        pk = carve(TOPK, SEQS)
        pden = carve(SEQS)
        gate = carve(TOPK, SEQS)
        idx_f = carve(TOPK, SEQS)
        oh = carve(TOPK, SEQS, E)
        hot = carve(SEQS, E)
        cnt_et = carve(E, SEQS)
        inc_et = carve(E, SEQS)
        seg = carve(E, SEQS)
        place = carve(SEQS, E)
        cmp_k = carve(E, SEQS)
        nt_e = carve(E)
        cum_e = carve(E)
        off_e = carve(E)
        cmp_t = carve(TILES, E)
        tile_f = carve(TILES)
        slot_f = carve(TOPK, SEQS)
        slot_i = carve(TOPK, SEQS).bitcast(I32)
        slot_a = carve(TOPK, SEQS).bitcast(I32)
        slot_b = carve(TOPK, SEQS).bitcast(I32)
        a_f = carve(TOPK, SEQS)
        b_f = carve(TOPK, SEQS)
        unused = carve(TILES)
        picked = carve(TOPK, SEQS, E)

        psum = [ctx.enter_context(nc.psum_tensor(f"bank{b}", [P, BANK], F32)) for b in range(8)]
        y_ps, a_ps, b_ps, o_ps = psum[0:ND], psum[4:4 + ABK], psum[6], psum[7]
        rank_ps, count_ps, order_ps = psum[3], psum[4], psum[5]
        up_ps, turn_ps, xturn_ps, down_ps = psum[0:2], psum[2:4], psum[6], psum[7]

        names = """ids_in weights_in setup_done ids_clean rows_clear a_bounded a_exp a_neg
            var1_ready rstd1_ready var2_ready rstd2_ready xn_ready xnT_ready in_ready step_ready
            conv_started conv_done xconv_ready zgate_ready proj_ready c_stored step_read step_logged dt_ready
            pool_turns dve_turns dtu_ready decay_ready b_ready dbu_ready scan_ready g_ready g_used y_ready yg_ready mix_ready
            h2_ready var3_ready rstd3_ready x2_ready x2_stored h2_stored x2_turned x2T_ready logits_ready
            logits_read mixer_done shifted expo_ready hot_ready ranks_ready order_ready onehots_ready lists_ready
            bias_in experts_ready from_ready xt_turned xT_ready up_ready biased hact_ready hid_turned
            hT0_ready hT1_ready down_ready yt_ready to_ready yt_added yt_free out_stored zero_stored
            dve_chain act_chain pool_chain""".split()
        s = {n: sem(n) for n in names}
        emb_in = [sem(f"emb_in{g}") for g in range(NG)]
        c_in = [sem(f"c_in{k}") for k in range(CSL)]
        e_in = [sem(f"expert_in{e}") for e in range(E)]
        x_in = [sem(f"xt_in{k}") for k in range(2)]

        def bc(ap, axis, *shape):
            return ap.unsqueeze(axis).broadcast_to([P, *shape])

        def seqs(ap):
            return ap.rearrange("p (s t) -> p s t", t=L)

        TURN0, TURN1, TURN2 = 5, 8, 11

        X_AT, Z_AT, P_AT, D_AT = KC, KC + ND, KC + 2 * ND, KC + 2 * ND + 1
        IN, STEP = KC + 2 * ND, 1 + ND

        def fbank(k):
            return psum[k % FB]

        def front(eng, inputs, steps, enter=None, leave=None):
            inputs(0)
            with eng.Fori(0, NG - 1) as g:
                if enter:
                    enter(g)
                inputs(g + 1)
                steps(g)
                if leave:
                    leave(NG - 1)
            steps(NG - 1)

        block = ctx.enter_context(nc.Block())

        @block.sync
        def _(sp):
            sp.dma_start(id_raw[:, :], ids).then_inc(s["ids_in"], 16)
            loads = [
                (lnw_sb, ln_w.rearrange("(k p) -> p k", p=P)), (lnb_sb, ln_b.rearrange("(k p) -> p k", p=P)),
                (win_sb, w_in.rearrange("(k p) e -> p k e", p=P)),
                (convw_sb, conv_w.rearrange("(k p) t -> p k t", p=P)),
                (convb_sb, conv_b.rearrange("(k p) -> p k", p=P)),
                (wxp_sb, w_xp.rearrange("(k p) e -> p k e", p=P)), (wdt_sb[0:R, :], w_dt),
                (bdt_sb, b_dt.rearrange("(k p) -> p k", p=P)),
                (a_sb, a_log.rearrange("(k p) n -> p k n", p=P)),
                (dskip_sb, d_skip.rearrange("(k p) -> p k", p=P)),
                (wout_sb, w_out.rearrange("(k p) c -> p k c", p=P)),
                (router_sb[:, :, :], w_router.rearrange("(k p) e -> p k e", p=P)),
            ]
            assert len(loads) == 12
            for dst, src in loads:
                sp.dma_start(dst, src, allow_slow_non_contiguous=True).then_inc(s["weights_in"], 16)
            sp.wait_ge(s["setup_done"], 1)
            sp.dma_start(sum_dram[NTOK:NTOK + P, :], zero_row[:, :]).then_inc(s["zero_stored"], 16)
            with sp.Fori(0, NG) as g:
                sp.wait_ge(s["proj_ready"], g + 1)
                sp.dma_start(c_dram[bass.ts(g, NS), :], projT[R + NS:PR, g, :]).then_inc(s["c_stored"], 16)
            sp.wait_ge(s["c_stored"], 16 * NG)
            sp.wait_ge(s["dt_ready"], 1 + ND * NG)

            def load_c(q, k):
                sp.dma_start(c_bc[:, k, :], c_dram[bass.ds(q, 1), :].broadcast_to([P, GW])).then_inc(c_in[k], 16)

            for k in range(CSL):
                load_c(k, k)
            with sp.Fori(1, NG * NS // CSL) as m:
                for k in range(CSL):
                    q = m * CSL + k
                    sp.wait_ge(s["g_ready"], ND + ND * (q - CSL + 1))
                    load_c(q, k)

            sp.wait_ge(s["mixer_done"], 1)
            for e in range(W2_EARLY):
                sp.dma_start(w1_sb[:, e, :, :], w1[e].rearrange("(k p) h -> p k h", p=P)).then_inc(e_in[e], 16)
                sp.dma_start(w2_sb[:, e, :, :], w2[e].rearrange("(k p) c -> p k c", p=P)).then_inc(e_in[e], 16)
                if e == 0:
                    sp.dma_start(b1_bc.rearrange("p e h -> p (e h)"),
                                 b1.rearrange("(a e) h -> a (e h)", a=1).broadcast_to([P, E * H])
                                 ).then_inc(s["bias_in"], 16)
                    sp.dma_start(b2_bc.rearrange("p e c -> p (e c)"),
                                 b2.rearrange("(a e) c -> a (e c)", a=1).broadcast_to([P, E * C])
                                 ).then_inc(s["bias_in"], 16)
            for e in range(W2_EARLY, E):
                sp.dma_start(w1_sb[:, e, :, :], w1[e].rearrange("(k p) h -> p k h", p=P)).then_inc(e_in[e], 16)
            sp.wait_ge(s["lists_ready"], 1)
            sp.wait_ge(s["x2_stored"], 16 * NG)
            for e in range(W2_EARLY, E):
                sp.dma_start(w2_sb[:, e, :, :], w2[e].rearrange("(k p) c -> p k c", p=P)).then_inc(e_in[e], 16)
            for e in range(E):
                sp.wait_ge(e_in[e], 32)
                sp.sem_inc(s["experts_ready"], 1)
            sp.wait_ge(s["yt_added"], 16 * TILES)
            sp.dma_start(out.rearrange("s t c -> (s t) c"), sum_dram[0:NTOK, :]).then_inc(s["out_stored"], 16)
            sp.wait_ge(s["out_stored"], 16)

        @block.gpsimd
        def _(pool):
            chain = Chain(pool, s["pool_chain"])
            pool.sem_inc(s["yt_free"], 2)
            pool.sem_inc(s["dt_ready"], 1)
            nc.gpsimd.memset(zero_row[:, :], 0.0).then_inc(s["setup_done"], 1)
            chain.then(nc.gpsimd.memset(ident[:, :], 0.0))
            chain.then(nc.gpsimd.memset(before[:, :], 1.0))
            chain.then(nc.gpsimd.memset(ones[:, :], 1.0))
            chain.then(nc.gpsimd.memset(power[:, :], -0.5))
            rows = [(iota_p, [[1, P]], 0, 0), (iota_k, [[P, SEQS]], 0, 0), (iota_t, [[1, TILES]], 0, 0),
                    (token, [[L, SEQS]], 0, 1), (spare, [[0, 1]], NTOK, 1)]
            for dst, pattern, base, per_partition in rows:
                chain.then(nc.gpsimd.iota(dst[:, :], pattern, base, per_partition,
                                          allow_small_or_imprecise_dtypes=True))
            chain.settle()
            nc.gpsimd.affine_select(out=ident[:, :], in_=ident[:, :], compare_op=ALU.not_equal, fill=1.0,
                                    base=0, pattern=[[-1, P]], channel_multiplier=1).then_inc(s["setup_done"], 1)
            nc.gpsimd.affine_select(out=before[:, :], in_=before[:, :], compare_op=ALU.is_gt, fill=0.0,
                                    base=0, pattern=[[1, P]], channel_multiplier=-1).then_inc(s["setup_done"], 1)
            pool.wait_ge(s["ids_clean"], 1)
            for i in range(SEQS):
                nc.gpsimd.indirect_dma_start(
                    out=h_res[:, i, :], out_offset=None, in_=emb_w,
                    in_offset=bass.IndirectOffsetOnAxis(ap=id_u[:, i:i + 1], axis=0)).then_inc(emb_in[i // GT], 16)

            pool.wait_ge(s["var1_ready"], 1)
            nc.gpsimd.tensor_tensor(rstd1[:, :], var1[:, :], power[:, :], ALU.pow).then_inc(s["rstd1_ready"], 1)

            def inputs(g):
                pool.wait_ge(s["var2_ready"], g + 1)
                nc.gpsimd.tensor_tensor(rstdg[:, :], varg[:, :], power[:, 0:GT], ALU.pow).then_inc(s["rstd2_ready"], 1)

            def past():
                pool.sem_inc(s["pool_turns"], 1)

            def steps(g):
                for d in range(ND):
                    k = d % 2
                    pool.wait_ge(s["step_logged"], g * ND + d + 1)
                    past()
                    chain.then(nc.gpsimd.tensor_scalar(sp_t[:, k, :], sp_e[:, k, :], 1.0, -1.0, ALU.add, ALU.add))
                    chain.settle()
                    past()
                    chain.then(nc.gpsimd.tensor_tensor(sp_t[:, k, :], sp_e[:, k, :], sp_t[:, k, :], ALU.subtract))
                    chain.settle()
                    past()
                    chain.then(nc.gpsimd.tensor_tensor(sp_t[:, k, :], sp_t[:, k, :], dt_sb[:, g, d, :], ALU.add))
                    chain.settle()
                    past()
                    nc.gpsimd.tensor_tensor(dt_sb[:, g, d, :], sp_t[:, k, :], sp_r[:, k, :],
                                            ALU.add).then_inc(s["dt_ready"], 1)

            inputs(0)
            inputs(1)
            with pool.Fori(0, NG - 2) as g:
                chain.enter(g, 3 * ND)
                inputs(g + 2)
                steps(g)
                chain.leave(NG - 2)
            steps(NG - 2)
            steps(NG - 1)

            pool.sem_inc(s["g_ready"], ND)

            def products(m):
                for k in range(CSL):
                    for d in range(ND):
                        u = (m * CSL + k) * ND + d
                        if d == 0:
                            pool.wait_ge(c_in[k], 16 * m + 16)
                        pool.wait_ge(s["scan_ready"], ABK + u + 1)
                        pool.wait_ge(s["g_used"], u + 1)
                        nc.gpsimd.tensor_tensor(g_buf[:, d, :], h_buf[:, d, :], c_bc[:, k, :],
                                                ALU.mult).then_inc(s["g_ready"], 1)

            def root(g):
                pool.wait_ge(s["var3_ready"], g + 1)
                nc.gpsimd.tensor_tensor(rstdh[:, :], varh[:, :], power[:, 0:GT], ALU.pow).then_inc(s["rstd3_ready"], 1)

            MG = NS // CSL
            with pool.Fori(0, MG) as m:
                products(m)
            with pool.Fori(1, NG) as g:
                products(g * MG)
                root(g - 1)
                with pool.Fori(1, MG) as m:
                    products(g * MG + m)
            root(NG - 1)

            def load_x(i, k, turned=True):
                pool.wait_ge(s["from_ready"], i + 1)
                if turned:
                    pool.wait_ge(s["xt_turned"], i - 1)
                past()
                nc.gpsimd.indirect_dma_start(
                    out=xt[:, k, :], out_offset=None, in_=x2_dram,
                    in_offset=bass.IndirectOffsetOnAxis(ap=from_u[k][:, :], axis=0)).then_inc(x_in[k], 16)

            def add_y(i, k, first=False):
                pool.wait_ge(s["to_ready"], i + 1)
                pool.wait_ge(s["yt_ready"], i + 2)
                if not first:
                    pool.wait_ge(s["yt_added"], 16 * i)
                    pool.sem_inc(s["yt_free"], 1)
                past()
                nc.gpsimd.indirect_dma_start(
                    out=sum_dram, out_offset=bass.IndirectOffsetOnAxis(ap=to_u[k][:, :], axis=0),
                    in_=yt[:, k, :], in_offset=None, compute_op=ALU.add).then_inc(s["yt_added"], 16)

            pool.wait_ge(s["x2_stored"], 16 * NG)
            load_x(0, 0, False)
            load_x(1, 1, False)
            load_x(2, 0)
            pool.wait_ge(s["h2_stored"], 16 * NG)
            pool.wait_ge(s["zero_stored"], 16)
            load_x(3, 1)
            add_y(0, 0, True)
            with pool.Fori(0, (TILES - 5) // 2) as m:
                for k in range(2):
                    load_x(2 * m + k + 4, k)
                    add_y(2 * m + k + 1, 1 - k)
            for i in range(TILES - 4, TILES):
                if i + 3 < TILES:
                    load_x(i + 3, (i + 3) % 2)
                add_y(i, i % 2)

        @block.scalar
        def _(act):
            chain = Chain(act, s["act_chain"])
            for ahead in ("xconv_ready", "step_read", "hT0_ready", "xT_ready"):
                act.sem_inc(s[ahead], 1)
            act.wait_ge(s["a_bounded"], 1)
            nc.scalar.activation(a_sb, a_sb, ACT.Exp).then_inc(s["a_exp"], 1)
            act.wait_ge(s["weights_in"], 16 * 12)
            act.wait_ge(s["rows_clear"], 1)

            def store_post(g):
                act.wait_ge(s["h2_ready"], g * GT + GT)
                act.dma_start(sum_dram[bass.ts(g, GW), :].rearrange("(j p) c -> p j c", p=P),
                              h_res[:, bass.ts(g, GT), :]).then_inc(s["h2_stored"], 16)
                act.wait_ge(s["x2_ready"], g * GT + GT)
                act.dma_start(x2_dram[bass.ts(g, GW), :].rearrange("(j p) c -> p j c", p=P),
                              x2).then_inc(s["x2_stored"], 16)

            def inputs(g):
                for c in range(KC):
                    act.wait_ge(s["in_ready"], g * IN + c + 1)
                    nc.scalar.activation(xnT[:, c, :], fbank(c)[:, :], ACT.Identity,
                                         bias=lnb_sb[:, c:c + 1], scale=lnw_sb[:, c:c + 1]).then_inc(s["xnT_ready"], 1)

                def conv_start(d):
                    act.wait_ge(s["xconv_ready"], 1 + g * ND + max(d - 1, 0))
                    act.wait_ge(s["in_ready"], g * IN + X_AT + d + 1)
                    nc.scalar.activation(conv_acc[:, d % 2, :], fbank(X_AT + d)[:, :], ACT.Identity,
                                         bias=convb_sb[:, d:d + 1],
                                         scale=convw_sb[:, d, TAPS - 1:TAPS]).then_inc(s["conv_started"], 1)

                def conv_end(d):
                    act.wait_ge(s["conv_done"], g * ND + d + 1)
                    nc.scalar.activation(xconv[:, g, d, :], conv_acc[:, d % 2, :],
                                         ACT.Silu).then_inc(s["xconv_ready"], 1)

                conv_start(0)
                for d in range(1, ND):
                    conv_start(d)
                    conv_end(d - 1)
                conv_end(ND - 1)
                for d in range(ND):
                    act.wait_ge(s["in_ready"], g * IN + Z_AT + d + 1)
                    nc.scalar.activation(zgate[:, g, d, :], fbank(Z_AT + d)[:, :],
                                         ACT.Silu).then_inc(s["zgate_ready"], 1)

            def steps(g):
                act.wait_ge(s["step_ready"], g * STEP + 1)
                nc.scalar.activation(projT[0:PR, g, :], fbank(P_AT)[0:PR, :], ACT.Copy).then_inc(s["proj_ready"], 1)
                for d in range(ND):
                    k = d % 2
                    bank = fbank(D_AT + d)
                    act.wait_ge(s["step_ready"], g * STEP + d + 2)
                    if d >= 2:
                        act.wait_ge(s["dt_ready"], 1 + g * ND + d - 1)
                    else:
                        act.wait_ge(s["dt_ready"], 1 + g * ND)
                    chain.then(nc.scalar.activation(sp_e[:, k, :], bank[:, :], ACT.Abs, bias=bdt_sb[:, d:d + 1]))
                    nc.scalar.activation(sp_r[:, k, :], bank[:, :], ACT.Relu,
                                         bias=bdt_sb[:, d:d + 1]).then_inc(s["step_read"], 1)
                    chain.settle()
                    chain.then(nc.scalar.activation(sp_e[:, k, :], sp_e[:, k, :], ACT.Exp, scale=-1.0))
                    chain.settle()
                    nc.scalar.activation(dt_sb[:, g, d, :], sp_e[:, k, :], ACT.Ln,
                                         bias=1.0).then_inc(s["step_logged"], 1)

            front(act, inputs, steps, lambda g: chain.enter(g, 2 * ND), chain.leave)

            act.wait_ge(s["a_neg"], 1)
            act.wait_ge(s["dt_ready"], 1 + ND * NG)

            def decays(g, n0, n1):
                with act.Fori(n0, n1) as n:
                    for d in range(ND):
                        u = (g * NS + n) * ND + d
                        act.wait_ge(s["scan_ready"], u + 1)
                        nc.scalar.activation(seqs(a_ps[d % ABK][:, :])[:, :, 1:L], seqs(dt_sb[:, g, d, :])[:, :, 1:L],
                                             ACT.Exp, scale=a_sb[:, d, bass.ds(n, 1)]).then_inc(s["decay_ready"], 1)

            def x2T_copy(g, half):
                act.wait_ge(s["x2_turned"], 2 * g + half + 1)
                nc.scalar.activation(x2T[:, bass.ts(half, BANK)], o_ps[:, :], ACT.Copy).then_inc(s["x2T_ready"], 1)

            decays(0, 0, NS)
            with act.Fori(1, NG) as g:
                decays(g, 0, TURN0 + 3)
                store_post(g - 1)
                x2T_copy(g - 1, 0)
                decays(g, TURN0 + 3, TURN1 + 3)
                x2T_copy(g - 1, 1)
                decays(g, TURN1 + 3, NS)
            store_post(NG - 1)
            x2T_copy(NG - 1, 0)
            x2T_copy(NG - 1, 1)

            act.wait_ge(s["shifted"], 1)
            nc.scalar.activation(ex, ex, ACT.Exp).then_inc(s["expo_ready"], 1)

            def xT_copy(i):
                act.wait_ge(s["xt_turned"], i + 1)
                nc.scalar.activation(xT[:, :], xturn_ps[:, 0:KC * P], ACT.Copy).then_inc(s["xT_ready"], 1)

            def gelu(i):
                for b in range(HB):
                    act.wait_ge(s["biased"], HB * i + b + 1)
                    nc.scalar.activation(hact[:, bass.ts(b, BANK)], up_ps[b][:, :],
                                         ACT.Gelu_apprx_tanh).then_inc(s["hact_ready"], 1)

            def hT_copy(i):
                act.wait_ge(s["hid_turned"], 2 * i + 1)
                nc.scalar.activation(hT[:, 0:BANK], turn_ps[0][:, :], ACT.Copy).then_inc(s["hT0_ready"], 1)

            xT_copy(0)
            gelu(0)
            xT_copy(1)
            with act.Fori(0, TILES - 2) as i:
                hT_copy(i)
                gelu(i + 1)
                xT_copy(i + 2)
            hT_copy(TILES - 2)
            gelu(TILES - 1)
            hT_copy(TILES - 1)

        @block.vector
        def _(dve):
            chain = Chain(dve, s["dve_chain"])
            for ahead in ("dbu_ready", "yg_ready", "hT1_ready", "yt_ready", "logits_read"):
                dve.sem_inc(s[ahead], 1)
            dve.wait_ge(s["ids_in"], 16)
            chain.then(nc.vector.tensor_copy(id_f[:, :], id_raw[:, :]))
            chain.settle()
            chain.then(nc.vector.tensor_scalar(id_c[:, :], id_f[:, :], 0.0, float(VOCAB - 1), ALU.max, ALU.min))
            chain.settle()
            nc.vector.tensor_copy(id_u[:, :], id_c[:, :]).then_inc(s["ids_clean"], 1)
            chain.then(nc.vector.tensor_tensor(id_ok[:, :], id_c[:, :], id_f[:, :], ALU.is_equal))
            nc.vector.memset(projT, 0.0).then_inc(s["rows_clear"], 1)
            dve.wait_ge(s["weights_in"], 16 * 12)
            nc.vector.tensor_scalar(a_sb, a_sb, A_LOG_MAX, None, ALU.min).then_inc(s["a_bounded"], 1)
            chain.settle()
            for i in range(SEQS):
                if i % GT == 0:
                    dve.wait_ge(emb_in[i // GT], 16 * GT)
                chain.then(nc.vector.tensor_scalar(h_res[:, i, :], h_res[:, i, :], id_ok[:, i:i + 1], None, ALU.mult))
                chain.settle()
                chain.then(nc.vector.bn_stats(st[:, i, :], h_res[:, i, :]))
            chain.settle()
            for i in range(SEQS):
                chain.then(nc.vector.bn_aggr(mv1[:, i, :], st[:, i, :]))
            chain.settle()
            nc.vector.tensor_scalar(var1[:, :], mv1[:, :, 1], EPS, None, ALU.add).then_inc(s["var1_ready"], 1)
            dve.wait_ge(s["a_exp"], 1)
            nc.vector.tensor_scalar(a_sb, a_sb, -1.0, None, ALU.mult).then_inc(s["a_neg"], 1)
            dve.wait_ge(s["rstd1_ready"], 1)

            def first_norm(dst, i):
                return nc.vector.tensor_scalar(dst, h_res[:, bass.ds(i, 1), :], mv1[:, bass.ds(i, 1), 0:1],
                                               rstd1[:, bass.ds(i, 1)], ALU.subtract, ALU.mult)

            def past():
                dve.sem_inc(s["dve_turns"], 1)

            def variances(g, mv, var, ready):
                past()
                for j in range(GT):
                    chain.then(nc.vector.bn_aggr(mv[:, j, :], st[:, j, :]))
                chain.settle()
                nc.vector.tensor_scalar(var[:, :], mv[:, :, 1], EPS, None, ALU.add).then_inc(s[ready], 1)

            def norms(g):
                if not (isinstance(g, int) and g == 0):
                    dve.wait_ge(s["in_ready"], (g - 1) * IN + KC)
                for j in range(GT):
                    chain.then(first_norm(xn4[:, j, :], g * GT + j))
                    chain.settle()
                    chain.then(nc.vector.bn_stats(st[:, j, :], xn4[:, j, :]))
                chain.settle()
                variances(g, mvg, varg, "var2_ready")
                dve.wait_ge(s["rstd2_ready"], g + 1)
                for j in range(GT):
                    nc.vector.tensor_scalar(xn4[:, j, :], xn4[:, j, :], mvg[:, j, 0:1], rstdg[:, j:j + 1],
                                            ALU.subtract, ALU.mult).then_inc(s["xn_ready"], 1)

            def convs(g):
                for d in range(ND):
                    dve.wait_ge(s["conv_started"], g * ND + d + 1)
                    x_ps, acc = seqs(fbank(X_AT + d)[:, :]), seqs(conv_acc[:, d % 2, :])
                    for back in range(1, TAPS):
                        ins = nc.vector.scalar_tensor_tensor(
                            out=acc[:, :, back:L], in0=x_ps[:, :, 0:L - back],
                            scalar=convw_sb[:, d, TAPS - 1 - back:TAPS - back], in1=acc[:, :, back:L],
                            op0=ALU.mult, op1=ALU.add)
                        if back < TAPS - 1:
                            chain.then(ins)
                            chain.settle()
                        else:
                            ins.then_inc(s["conv_done"], 1)

            front(dve, norms, convs, lambda g: chain.enter(g, 3 * GT + (TAPS - 2) * ND), chain.leave)

            dve.wait_ge(s["dt_ready"], 1 + ND * NG)
            for k in range(ABK):
                nc.vector.memset(seqs(a_ps[k][:, :])[:, :, 0:1], 0.0).then_inc(s["scan_ready"], 1)

            def inputs(g):
                for d in range(ND):
                    nc.vector.tensor_tensor(dtu[:, d, :], dt_sb[:, g, d, :], xconv[:, g, d, :],
                                            ALU.mult).then_inc(s["dtu_ready"], 1)

            def step(g, n):
                q = g * NS + n

                def input_of(d):
                    if d == 0:
                        dve.wait_ge(s["dtu_ready"], g * ND + ND)
                        dve.wait_ge(s["b_ready"], q + 1)
                    nc.vector.tensor_tensor(dbu[:, d, :], dtu[:, d, :], b_ps[:, :], ALU.mult
                                            ).then_inc(s["dbu_ready"], 1)

                def scan_of(d):
                    u = q * ND + d
                    dve.wait_ge(s["decay_ready"], u + 1)
                    dve.wait_ge(s["dbu_ready"], 1 + u + 1)
                    dve.wait_ge(s["g_ready"], u + 1)
                    nc.vector.tensor_tensor_scan(h_buf[:, d, :], a_ps[d % ABK][:, :], dbu[:, d, :], 0.0,
                                                 ALU.mult, ALU.add).then_inc(s["scan_ready"], 1)

                input_of(0)
                for d in range(1, ND):
                    input_of(d)
                    scan_of(d - 1)
                scan_of(ND - 1)

            def gated(g):
                for d in range(ND):
                    dve.wait_ge(s["y_ready"], g * ND + d + 1)
                    chain.then(nc.vector.scalar_tensor_tensor(
                        out=yg[:, d, :], in0=xconv[:, g, d, :], scalar=dskip_sb[:, d:d + 1], in1=y_ps[d][:, :],
                        op0=ALU.mult, op1=ALU.add))
                    chain.settle()
                    nc.vector.tensor_tensor(yg[:, d, :], yg[:, d, :], zgate[:, g, d, :],
                                            ALU.mult).then_inc(s["yg_ready"], 1)

            def mixed(g, half):
                for j in (2 * half, 2 * half + 1):
                    i = g * GT + j
                    chain.then(first_norm(x1tmp[:, j % 2, :], i))
                    chain.settle()
                    chain.then(nc.vector.tensor_tensor(h_res[:, bass.ds(i, 1), :], h_res[:, bass.ds(i, 1), :],
                                                       x1tmp[:, j % 2:j % 2 + 1, :], ALU.add))
                chain.settle()
                dve.wait_ge(s["mix_ready"], 2 * g + half + 1)
                for j in (2 * half, 2 * half + 1):
                    i = g * GT + j
                    nc.vector.tensor_tensor(h_res[:, bass.ds(i, 1), :], h_res[:, bass.ds(i, 1), :],
                                            o_ps[:, bass.ts(j % 2, C)].unsqueeze(1), ALU.add
                                            ).then_inc(s["h2_ready"], 1)
                dve.wait_ge(s["h2_ready"], g * GT + 2 * half + 2)
                past()
                for j in (2 * half, 2 * half + 1):
                    chain.then(nc.vector.bn_stats(st[:, j, :], h_res[:, bass.ds(g * GT + j, 1), :]))
                chain.settle()

            def third_norm(g):
                if not (isinstance(g, int) and g == 0):
                    dve.wait_ge(s["x2_stored"], g * 16)
                    dve.wait_ge(s["x2_turned"], g * 2)
                dve.wait_ge(s["rstd3_ready"], g + 1)
                for j in range(GT):
                    nc.vector.tensor_scalar(x2[:, j, :], h_res[:, bass.ds(g * GT + j, 1), :], mvh[:, j, 0:1],
                                            rstdh[:, j:j + 1], ALU.subtract, ALU.mult).then_inc(s["x2_ready"], 1)

            def logits_copy(g):
                dve.wait_ge(s["logits_ready"], g + 1)
                nc.vector.tensor_scalar(lg[:, bass.ts(g, GT), :], o_ps[:, 0:GT * E].rearrange("p (i e) -> p i e", e=E),
                                        1.0, None, ALU.mult).then_inc(s["logits_read"], 1)

            inputs(0)
            with dve.Fori(0, NS) as n:
                step(0, n)
            with dve.Fori(1, NG) as g:
                chain.enter(g - 1, ND + 6 * 2 + GT)
                inputs(g)
                step(g, 0)
                gated(g - 1)
                step(g, 1)
                mixed(g - 1, 0)
                step(g, 2)
                mixed(g - 1, 1)
                variances(g - 1, mvh, varh, "var3_ready")
                step(g, 3)
                step(g, 4)
                third_norm(g - 1)
                with dve.Fori(5, NS - 1) as n:
                    step(g, n)
                logits_copy(g - 1)
                step(g, NS - 1)
                chain.leave(NG - 1)
            gated(NG - 1)
            mixed(NG - 1, 0)
            mixed(NG - 1, 1)
            dve.sem_inc(s["mixer_done"], 1)
            variances(NG - 1, mvh, varh, "var3_ready")
            third_norm(NG - 1)
            logits_copy(NG - 1)

            dve.wait_ge(s["logits_read"], 1 + NG)
            for i in range(SEQS):
                chain.then(nc.vector.max(top8[:, i, :], lg[:, i, :]))
            chain.settle()
            nc.vector.tensor_tensor(ex, lg[:, :, :], top8[:, :, 0:1].broadcast_to([P, SEQS, E]),
                                    ALU.subtract).then_inc(s["shifted"], 1)
            for i in range(SEQS):
                chain.then(nc.vector.max_index(idx8[:, i, :], top8[:, i, :], lg[:, i, :]))
            chain.settle()
            for j in range(TOPK):
                chain.then(nc.vector.tensor_copy(idx_f[:, j, :], idx8[:, :, j]))
            chain.settle()
            for j in range(TOPK):
                chain.then(nc.vector.tensor_tensor(oh[:, j, :, :], bc(idx_f[:, j, :], 2, SEQS, E),
                                                   bc(iota_p[:, 0:E], 1, SEQS, E), ALU.is_equal))
            chain.settle()
            nc.vector.tensor_tensor(hot, oh[:, 0, :, :], oh[:, 1, :, :], ALU.add).then_inc(s["hot_ready"], 1)
            dve.wait_ge(s["expo_ready"], 1)
            chain.then(nc.vector.reduce_sum(ssum, ex, AX_X))
            for j in range(TOPK):
                chain.then(nc.vector.tensor_tensor(picked[:, j, :, :], oh[:, j, :, :], ex, ALU.mult))
            chain.settle()
            chain.then(nc.vector.reciprocal(rsum, ssum))
            for j in range(TOPK):
                chain.then(nc.vector.reduce_sum(pk[:, j, :], picked[:, j, :, :], AX_X))
            chain.settle()
            for j in range(TOPK):
                chain.then(nc.vector.tensor_tensor(pk[:, j, :], pk[:, j, :], rsum, ALU.mult))
            chain.settle()
            chain.then(nc.vector.tensor_tensor(pden, pk[:, 0, :], pk[:, 1, :], ALU.add))
            chain.settle()
            chain.then(nc.vector.tensor_scalar(pden, pden, 1e-8, None, ALU.add))
            chain.settle()
            chain.then(nc.vector.reciprocal(pden, pden))
            chain.settle()
            for j in range(TOPK):
                chain.then(nc.vector.tensor_tensor(gate[:, j, :], pk[:, j, :], pden, ALU.mult))

            dve.wait_ge(s["ranks_ready"], 1)
            chain.then(nc.vector.tensor_copy(cnt_et, count_ps[:, 0:SEQS * E].rearrange("p (i e) -> p e i", e=E)))
            chain.then(nc.vector.memset(seg, 1.0))
            chain.settle()
            chain.then(nc.vector.memset(seg[:, :, 0:1], 0.0))
            chain.settle()
            chain.then(nc.vector.tensor_tensor_scan(
                inc_et.rearrange("p e i -> p (e i)"), seg.rearrange("p e i -> p (e i)"),
                cnt_et.rearrange("p e i -> p (e i)"), 0.0, ALU.mult, ALU.add))
            chain.settle()
            chain.then(nc.vector.tensor_tensor(cmp_k, inc_et[:, :, SEQS - 1:SEQS].broadcast_to([P, E, SEQS]),
                                               bc(iota_k[:, :], 1, E, SEQS), ALU.is_gt))
            chain.settle()
            chain.then(nc.vector.reduce_sum(nt_e, cmp_k, AX_X))
            chain.settle()
            chain.then(nc.vector.tensor_tensor_scan(cum_e, ones[:, 0:E], nt_e, 0.0, ALU.mult, ALU.add))
            chain.settle()
            chain.then(nc.vector.tensor_tensor(off_e, cum_e, nt_e, ALU.subtract))
            chain.then(nc.vector.tensor_tensor(cmp_t, bc(cum_e, 1, TILES, E), bc(iota_t[:, :], 2, TILES, E), ALU.is_le))
            chain.settle()
            chain.then(nc.vector.tensor_scalar(off_e, off_e, float(P), None, ALU.mult))
            chain.then(nc.vector.reduce_sum(tile_f, cmp_t, AX_X))
            chain.settle()
            chain.then(nc.vector.tensor_scalar(tile_e[:, :], tile_f, float(E - 1), None, ALU.min))
            chain.then(nc.vector.tensor_tensor(inc_et, inc_et, cnt_et, ALU.subtract))
            chain.settle()
            chain.then(nc.vector.tensor_tensor(inc_et, inc_et, bc(off_e, 2, E, SEQS), ALU.add))
            chain.settle()
            chain.then(nc.vector.tensor_tensor(place, rank_ps[:, 0:SEQS * E].rearrange("p (i e) -> p i e", e=E),
                                               inc_et.rearrange("p e i -> p i e"), ALU.add))
            chain.settle()
            for j in range(TOPK):
                chain.then(nc.vector.tensor_tensor(picked[:, j, :, :], oh[:, j, :, :], place, ALU.mult))
            chain.settle()
            for j in range(TOPK):
                chain.then(nc.vector.reduce_sum(slot_f[:, j, :], picked[:, j, :, :], AX_X))
            chain.settle()
            chain.then(nc.vector.tensor_copy(slot_i, slot_f))
            chain.settle()
            chain.then(nc.vector.tensor_scalar(slot_a, slot_i, P.bit_length() - 1, None, ALU.arith_shift_right))
            chain.then(nc.vector.tensor_scalar(slot_b, slot_i, P - 1, None, ALU.bitwise_and))
            chain.settle()
            chain.then(nc.vector.tensor_copy(a_f, slot_a))
            chain.then(nc.vector.tensor_copy(b_f, slot_b))
            chain.settle()
            for j in range(TOPK):
                tiles_of = to_add[:, j * SEQS:(j + 1) * SEQS, :, :]
                chain.then(nc.vector.tensor_tensor(tiles_of[:, :, 2, :], bc(iota_t[:, :], 1, SEQS, TILES),
                                                   bc(a_f[:, j, :], 2, SEQS, TILES), ALU.is_equal))
            chain.settle()
            for j in range(TOPK):
                tiles_of = to_add[:, j * SEQS:(j + 1) * SEQS, :, :]
                chain.then(nc.vector.tensor_tensor(tiles_of[:, :, 0, :], tiles_of[:, :, 2, :],
                                                   bc(token[:, :], 2, SEQS, TILES), ALU.mult))
                nc.vector.tensor_tensor(tiles_of[:, :, 1, :], tiles_of[:, :, 2, :],
                                        bc(gate[:, j, :], 2, SEQS, TILES), ALU.mult).then_inc(s["onehots_ready"], 1)
            chain.settle()
            for r in range(TOPK * SEQS):
                nc.vector.tensor_scalar(hot_b[:, r, :], iota_p[:, :], b_f[:, r // SEQS, r % SEQS:r % SEQS + 1], None,
                                        ALU.is_equal).then_inc(s["onehots_ready"], 1)
            dve.wait_ge(s["order_ready"], 1)
            chain.then(nc.vector.tensor_copy(from_t[:, :], order_ps[:, 0:TILES]))
            chain.then(nc.vector.tensor_copy(gate_t[:, :], order_ps[:, TILES:2 * TILES]))
            chain.then(nc.vector.tensor_scalar(unused, order_ps[:, 2 * TILES:3 * TILES], -1.0, 1.0, ALU.mult, ALU.add))
            chain.settle()
            chain.then(nc.vector.scalar_tensor_tensor(out=to_t[:, :], in0=unused, scalar=spare[:, 0:1],
                                                      in1=from_t[:, :], op0=ALU.mult, op1=ALU.add))
            chain.settle()
            dve.sem_inc(s["lists_ready"], 1)

            def from_index(i, k):
                nc.vector.tensor_scalar(from_u[k][:, :], from_t[:, bass.ds(i, 1)], 1.0, None,
                                        ALU.mult).then_inc(s["from_ready"], 1)

            def bias_up(i):
                e = dve.value_load(tile_e[0:1, bass.ds(i, 1)], min_val=0, max_val=E - 1)
                for b in range(HB):
                    dve.wait_ge(s["up_ready"], HB * i + b + 1)
                    nc.vector.tensor_tensor(up_ps[b][:, :], up_ps[b][:, :],
                                            b1_bc[:, bass.ds(e, 1), bass.ts(b, BANK)], ALU.add
                                            ).then_inc(s["biased"], 1)

            def hT_copy(i):
                dve.wait_ge(s["hid_turned"], 2 * i + 2)
                nc.vector.tensor_copy(hT[:, BANK:2 * BANK], turn_ps[1][:, :]).then_inc(s["hT1_ready"], 1)

            def weigh(i, k, chained):
                e = dve.value_load(tile_e[0:1, bass.ds(i, 1)], min_val=0, max_val=E - 1)
                dve.wait_ge(s["yt_free"], i + 1)
                nc.vector.tensor_scalar(to_u[k][:, :], to_t[:, bass.ds(i, 1)], 1.0, None,
                                        ALU.mult).then_inc(s["to_ready"], 1)
                dve.wait_ge(s["down_ready"], i + 1)
                chained.then(nc.vector.tensor_tensor(yt[:, k, :], down_ps[:, 0:C], b2_bc[:, bass.ds(e, 1), :], ALU.add))
                chained.settle()
                nc.vector.tensor_scalar(yt[:, k, :], yt[:, k, :], gate_t[:, bass.ds(i, 1)], None,
                                        ALU.mult).then_inc(s["yt_ready"], 1)

            from_index(0, 0)
            from_index(1, 1)
            dve.wait_ge(s["bias_in"], 32)
            bias_up(0)
            dve.wait_ge(x_in[0], 16)
            from_index(2, 0)
            with dve.Fori(0, (TILES - 3) // 2) as m:
                chain.enter(m, 2)
                for k in range(2):
                    i = 2 * m + k
                    dve.wait_ge(x_in[1 - k], 16 * m + 16 + 16 * k)
                    from_index(i + 3, 1 - k)
                    hT_copy(i)
                    bias_up(i + 1)
                    weigh(i, k, chain)
                chain.leave((TILES - 3) // 2)
            for i in range(TILES - 3, TILES):
                hT_copy(i)
                if i + 1 < TILES:
                    bias_up(i + 1)
                weigh(i, i % 2, chain)

        @block.tensor
        def _(pe):
            def mm(dst, lhsT, rhs, first=True, last=True):
                return nc.tensor.matmul(dst, lhsT, rhs, start=first, stop=last)

            pe.wait_ge(s["setup_done"], 3)
            pe.wait_ge(s["weights_in"], 16 * 12)

            def inputs(g):
                if not (isinstance(g, int) and g == 0):
                    pe.wait_ge(s["step_read"], 1 + (g - 1) * ND)
                    pe.wait_ge(s["zgate_ready"], g * ND)
                pe.wait_ge(s["xn_ready"], g * GT + GT)
                for c in range(KC):
                    for j in range(GT):
                        ins = nc.tensor.transpose(fbank(c)[:, bass.ts(j, P)], xn4[:, j, bass.ts(c, P)], ident[:, :])
                    ins.then_inc(s["in_ready"], 1)
                pe.wait_ge(s["xnT_ready"], g * KC + KC)
                for d in range(2 * ND):
                    k = X_AT + d
                    last_use = k - FB
                    if last_use >= Z_AT:
                        pe.wait_ge(s["zgate_ready"], g * ND + last_use - Z_AT + 1)
                    elif last_use >= X_AT:
                        pe.wait_ge(s["conv_done"], g * ND + last_use - X_AT + 1)
                    for c in range(KC):
                        ins = mm(fbank(k)[:, :], win_sb[:, c, bass.ts(d, P)], xnT[:, c, :], c == 0, c == KC - 1)
                    ins.then_inc(s["in_ready"], 1)

            def steps(g):
                later = g + 1 if not isinstance(g, int) else NG - 1
                pe.wait_ge(s["xconv_ready"], 1 + g * ND + ND)
                pe.wait_ge(s["zgate_ready"], later * ND + P_AT - FB - Z_AT + 1)
                if isinstance(g, int):
                    pe.wait_ge(s["step_read"], 1 + g * ND)
                for d in range(ND):
                    ins = mm(fbank(P_AT)[0:PR, :], wxp_sb[:, d, :], xconv[:, g, d, :], d == 0, d == ND - 1)
                ins.then_inc(s["step_ready"], 1)
                pe.wait_ge(s["zgate_ready"], later * ND + ND)
                pe.wait_ge(s["proj_ready"], g + 1)
                for d in range(ND):
                    mm(fbank(D_AT + d)[:, :], wdt_sb[0:R, bass.ts(d, P)], projT[0:R, g, :]
                       ).then_inc(s["step_ready"], 1)

            front(pe, inputs, steps)

            pe.sem_inc(s["g_used"], ND)
            pe.wait_ge(s["dt_ready"], 1 + ND * NG)

            def b_row(g, n):
                pe.wait_ge(s["dbu_ready"], 1 + (g * NS + n) * ND)
                mm(b_ps[:, :], ident[:, R + n:R + n + 1].broadcast_to([P, P]),
                   projT[:, g, :]).then_inc(s["b_ready"], 1)

            def y_add(g, n):
                for d in range(ND):
                    if n == 0 and d == 0:
                        pe.wait_ge(s["yg_ready"], 1 + g * ND)
                    pe.wait_ge(s["g_ready"], ND + (g * NS + n) * ND + d + 1)
                    mm(y_ps[d][:, :], ident[:, :], g_buf[:, d, :], n == 0, n == NS - 1).then_inc(s["g_used"], 1)

            def y_tell(g):
                for d in range(ND):
                    pe.wait_ge(s["g_used"], ND + (g * NS + NS - 1) * ND + d + 1)
                    pe.sem_inc(s["y_ready"], 1)

            def mix(g, half):
                if half == 0:
                    pe.wait_ge(s["yg_ready"], 1 + g * ND + ND)
                    pe.wait_ge(s["logits_read"], 1 + g)
                else:
                    pe.wait_ge(s["h2_ready"], g * GT + 2)
                for j in (2 * half, 2 * half + 1):
                    for d in range(ND):
                        ins = mm(o_ps[:, bass.ts(j % 2, C)], yg[:, d, bass.ts(j, P)], wout_sb[:, d, :],
                                 d == 0, d == ND - 1)
                ins.then_inc(s["mix_ready"], 1)

            def turn(g, half):
                if half == 0:
                    pe.wait_ge(s["x2_ready"], g * GT + GT)
                else:
                    pe.wait_ge(s["x2T_ready"], 2 * g + 1)
                for j in (2 * half, 2 * half + 1):
                    for c in range(KC):
                        ins = nc.tensor.transpose(o_ps[:, bass.ts((j % 2) * KC + c, P)], x2[:, j, bass.ts(c, P)],
                                                  ident[:, :])
                ins.then_inc(s["x2_turned"], 1)

            def logits(g):
                pe.wait_ge(s["x2T_ready"], 2 * g + 2)
                for j in range(GT):
                    for c in range(KC):
                        ins = mm(o_ps[:, bass.ts(j, E)], x2T[:, bass.ts(j * KC + c, P)], router_sb[:, c, :],
                                 c == 0, c == KC - 1)
                ins.then_inc(s["logits_ready"], 1)

            def scan_group(g, post):
                b_row(g, 0)
                for n in range(NS):
                    if n + 1 < NS:
                        b_row(g, n + 1)
                    y_add(g, n)
                    if post and n == 0:
                        mix(g - 1, 0)
                    if post and n == 1:
                        mix(g - 1, 1)
                    if post and n == TURN0:
                        turn(g - 1, 0)
                    if post and n == TURN1:
                        turn(g - 1, 1)
                    if post and n == TURN2:
                        logits(g - 1)
                y_tell(g)

            scan_group(0, False)
            with pe.Fori(1, NG) as g:
                scan_group(g, True)
            mix(NG - 1, 0)
            mix(NG - 1, 1)
            turn(NG - 1, 0)
            turn(NG - 1, 1)
            logits(NG - 1)

            pe.wait_ge(s["hot_ready"], 1)
            mm(rank_ps[:, 0:SEQS * E], before[:, :], hot.rearrange("p i e -> p (i e)"))
            mm(count_ps[:, 0:SEQS * E], ones[:, :], hot.rearrange("p i e -> p (i e)")).then_inc(s["ranks_ready"], 1)
            for r in range(TOPK * SEQS):
                pe.wait_ge(s["onehots_ready"], TOPK + r + 1)
                ins = mm(order_ps[:, 0:3 * TILES], hot_b[:, r, :], to_add[:, r, :, :].rearrange("p a t -> p (a t)"),
                         r == 0, r == TOPK * SEQS - 1)
            ins.then_inc(s["order_ready"], 1)
            pe.wait_ge(s["lists_ready"], 1)

            def turn_x(i, k, m):
                pe.wait_ge(x_in[k], 16 * m + 16)
                pe.wait_ge(s["xT_ready"], 1 + i)
                for c in range(KC):
                    ins = nc.tensor.transpose(xturn_ps[:, bass.ts(c, P)], xt[:, k, bass.ts(c, P)], ident[:, :])
                ins.then_inc(s["xt_turned"], 1)

            def up(i):
                e = pe.value_load(tile_e[0:1, bass.ds(i, 1)], min_val=0, max_val=E - 1)
                pe.wait_ge(s["experts_ready"], e + 1)
                pe.wait_ge(s["xT_ready"], 1 + i + 1)
                for b in range(HB):
                    for c in range(KC):
                        ins = mm(up_ps[b][:, :], xT[:, bass.ts(c, P)],
                                 w1_sb[:, bass.ds(e, 1), c, bass.ts(b, BANK)], c == 0, c == KC - 1)
                    ins.then_inc(s["up_ready"], 1)

            def turn_h(i):
                for b in range(2):
                    pe.wait_ge(s["hact_ready"], HB * i + b + 1)
                    pe.wait_ge(s[("hT0_ready", "hT1_ready")[b]], 1 + i)
                    for j in range(4):
                        ins = nc.tensor.transpose(turn_ps[b][:, bass.ts(j, P)], hact[:, bass.ts(4 * b + j, P)],
                                                  ident[:, :])
                    ins.then_inc(s["hid_turned"], 1)

            def down(i):
                e = pe.value_load(tile_e[0:1, bass.ds(i, 1)], min_val=0, max_val=E - 1)
                pe.wait_ge(s["yt_ready"], 1 + i)
                pe.wait_ge(s["hT0_ready"], 1 + i + 1)
                pe.wait_ge(s["hT1_ready"], 1 + i + 1)
                for h in range(KH):
                    ins = mm(down_ps[:, 0:C], hT[:, bass.ts(h, P)], w2_sb[:, bass.ds(e, 1), h, :],
                             h == 0, h == KH - 1)
                ins.then_inc(s["down_ready"], 1)

            turn_x(0, 0, 0)
            up(0)
            turn_x(1, 1, 0)
            with pe.Fori(0, (TILES - 3) // 2) as m:
                for k in range(2):
                    i = 2 * m + k
                    turn_h(i)
                    up(i + 1)
                    turn_x(i + 2, k, m + 1)
                    down(i)
            for i in range(TILES - 3, TILES):
                turn_h(i)
                if i + 1 < TILES:
                    up(i + 1)
                if i + 2 < TILES:
                    turn_x(i + 2, i % 2, i // 2 + 1)
                down(i)


def kernel(x, L0_tok_embedding, L0_attn_ln_w, L0_attn_ln_b, L0_attn_W_in, L0_attn_conv_w, L0_attn_conv_b,
           L0_attn_W_xproj, L0_attn_W_dt, L0_attn_b_dt, L0_attn_A_log, L0_attn_Dskip, L0_attn_W_out,
           L0_ffn_router_w, L0_ffn_w1, L0_ffn_b1, L0_ffn_w2, L0_ffn_b2):
    import numpy as _np
    import concourse.bacc as _bacc
    from concourse import mybir as _mybir
    from concourse.bass_utils import run_bass_kernel_spmd as _run

    given = {
        "ids": x.T, "embedding": L0_tok_embedding, "ln_w": L0_attn_ln_w, "ln_b": L0_attn_ln_b,
        "w_in": L0_attn_W_in.T, "conv_w": L0_attn_conv_w, "conv_b": L0_attn_conv_b,
        "w_xproj": L0_attn_W_xproj.T, "w_dt": L0_attn_W_dt.T, "b_dt": L0_attn_b_dt, "a_log": L0_attn_A_log,
        "d_skip": L0_attn_Dskip, "w_out": L0_attn_W_out.T, "router": L0_ffn_router_w.T,
        "w1": L0_ffn_w1.transpose(0, 2, 1), "b1": L0_ffn_b1, "w2": L0_ffn_w2.transpose(0, 2, 1), "b2": L0_ffn_b2,
    }
    nc = _bacc.Bacc("TRN2", target_bir_lowering=False, num_devices=1)
    arrays, args = {}, []
    for name, a in given.items():
        a = _np.ascontiguousarray(a)
        arrays[f"in_{name}"] = a
        args.append(nc.dram_tensor(f"in_{name}", a.shape, _mybir.dt.from_np(a.dtype), kind="ExternalInput").ap())
    seqs, length = x.shape
    shape = (seqs, length, L0_tok_embedding.shape[1])
    args.append(nc.dram_tensor("out", shape, _mybir.dt.float32, kind="ExternalOutput").ap())
    tower_kernel(nc, *args)
    r = _run(nc, [arrays], core_ids=[0])
    return r.results[0]["out"]
```

```python
from contextlib import ExitStack

import concourse.bass as bass
from concourse import mybir

ALU = mybir.AluOpType
ACT = mybir.ActivationFunctionType
F32 = mybir.dt.float32
F32R = mybir.dt.float32r
I32 = mybir.dt.int32
U32 = mybir.dt.uint32
AX_X = mybir.AxisListType.X


class Chain:

    def __init__(self, eng, sem):
        self.eng, self.sem, self.base, self.local = eng, sem, 0, 0

    def then(self, ins):
        ins.then_inc(self.sem, 1)
        self.local += 1

    def settle(self):
        self.eng.wait_ge(self.sem, self.base + self.local)

    def enter(self, turn, per_turn):
        self.start, self.per_turn = self.base + self.local, per_turn
        self.base, self.local = self.start + turn * per_turn, 0

    def leave(self, turns):
        assert self.local == self.per_turn, (self.local, self.per_turn)
        self.base, self.local = self.start + turns * self.per_turn, 0


def tower_kernel(nc, ids, emb_w, ln_w, ln_b, w_in, conv_w, conv_b, w_xp, w_dt, b_dt, a_log, d_skip,
                 w_out, w_router, w1, b1, w2, b2, out):
    P = 128
    VOCAB, C = emb_w.shape
    L, SEQS = ids.shape
    NTOK = SEQS * L
    DI = w_out.shape[0]
    NS = a_log.shape[1]
    R = w_dt.shape[0]
    PR = w_xp.shape[1]
    TAPS = conv_w.shape[1]
    E, _, H = w1.shape
    KC, ND, KH = C // P, DI // P, H // P
    GT = 4
    NG = SEQS // GT
    GW = GT * L
    TOPK = 2
    TILES = (TOPK * NTOK + E * (P - 1)) // P
    BANK = 512
    HB = H // BANK
    EPS = 1e-5
    A_LOG_MAX = 84.0
    CSL = 4
    ASL = 4
    NR = 3
    NT = ND - NR
    LOADS = 13
    HALF = 64
    HIGH = -(1 << 12)
    assert L == P and PR == R + 2 * NS and TILES % 2 == 1 and ND == CSL == GT and GW == BANK

    c_dram = nc.dram_tensor("c_rows", [NG * NS, GW], F32).ap()
    x2_dram = nc.dram_tensor("expert_in", [NTOK, C], F32).ap()
    sum_dram = nc.dram_tensor("sums", [NTOK + P, C], F32).ap()

    ctx = ExitStack()
    with ctx:
        def sb(name, shape, dt=F32):
            return ctx.enter_context(nc.sbuf_tensor(name, shape, dt))

        def sem(name):
            return ctx.enter_context(nc.semaphore(name))

        ident = sb("ident", [P, P])
        before = sb("before", [P, P])
        ones = sb("ones", [P, P])
        iota_p = sb("iota_p", [P, P])
        iota_k = sb("iota_k", [P, SEQS])
        iota_t = sb("iota_t", [P, TILES])
        token = sb("token", [P, SEQS])
        spare = sb("spare", [P, 1])
        power = sb("power", [P, SEQS])
        h_res = sb("h_res", [P, SEQS, C])
        st = sb("st", [P, GT, 6])
        mean1 = sb("mean1", [P, SEQS])
        mvf = sb("mvf", [P, GT, 2])
        mvg = sb("mvg", [P, GT, 2])
        mvh = sb("mvh", [P, GT, 2])
        varf = sb("varf", [P, GT])
        varg = sb("varg", [P, GT])
        varh = sb("varh", [P, GT])
        rstd1 = sb("rstd1", [P, SEQS])
        rstdf = sb("rstdf", [P, GT])
        rstdg = sb("rstdg", [P, GT])
        rstdh = sb("rstdh", [P, GT])
        id_raw = sb("id_raw", [P, SEQS], I32)
        id_f = sb("id_f", [P, SEQS])
        id_c = sb("id_c", [P, SEQS])
        id_ok = sb("id_ok", [P, SEQS])
        id_u = sb("id_u", [P, SEQS], U32)
        lg = sb("lg", [P, SEQS, E])
        gate_t = sb("gate_t", [P, TILES])
        from_t = sb("from_t", [P, TILES])
        to_t = sb("to_t", [P, TILES])
        from_u = [sb(f"from_u{k}", [P, 1], U32) for k in range(2)]
        to_u = [sb(f"to_u{k}", [P, 1], U32) for k in range(2)]
        tile_e = sb("tile_e", [P, TILES], I32)
        router_sb = sb("router_sb", [P, KC, E])
        xt = sb("xt", [P, 2, C])
        xT = sb("xT", [P, KC * P])
        hact = sb("hact", [P, H])
        hT = sb("hT", [P, KH * P])
        yt = sb("yt", [P, 2, C])
        proj_hl = sb("proj_hl", [P, NG, GW], F32R)
        pick_b = sb("pick_b", [P, NS], F32R)
        warm = sb("warm", [P, 1])
        zero_row = sb("zero_row", [P, C])

        psum = [ctx.enter_context(nc.psum_tensor(f"bank{b}", [P, BANK], F32)) for b in range(8)]

        WORDS = 160 * 256
        arena = sb("arena", [P, WORDS])
        at = [0]

        def carve(*shape):
            size = 1
            for n in shape:
                size *= n
            v = arena[:, at[0]:at[0] + size]
            at[0] += size
            assert at[0] <= WORDS, at
            if len(shape) == 2:
                v = v.rearrange("p (a b) -> p a b", b=shape[1])
            elif len(shape) == 3:
                v = v.rearrange("p (a b c) -> p a b c", b=shape[1], c=shape[2])
            return v

        xconv = carve(NG, ND, GW)
        zgate = carve(NG, ND, GW)
        dt_sb = carve(NG, ND, GW)
        wxp_sb = carve(ND, P)
        wdt_sb = carve(DI)
        wout_sb = carve(ND, C)
        lnw_sb = carve(KC)
        lnb_sb = carve(KC)
        convw_sb = carve(ND, TAPS)
        convb_sb = carve(ND)
        bdt_sb = carve(ND)
        a_sb = carve(ND, NS)
        dskip_sb = carve(ND)
        bT = carve(GT, NG * NS)
        dtu = carve(ND, GW)
        x1tmp = carve(2, C)
        x2 = carve(GT, C)
        x1 = x2
        front_at = at[0]
        win_sb = carve(KC, 2 * DI)
        xnT = carve(KC, GW)
        conv_acc = carve(ND, GW)
        sp_e = carve(ND, GW)
        sp_t = dtu
        sp_r = carve(ND, GW)
        at[0] = front_at
        h_buf = carve(ND, GW)
        dbu2 = carve(2, GW)
        decay_own = carve(GW)
        g_buf = carve(ND, GW)
        c_bc = carve(CSL, GW)
        yg = carve(ND, GW)
        x2T = hact[:, :]
        proj_hi = yt[:, :, :].rearrange("p k c -> p (k c)")
        dtuT = hT[:, 0:GT * NT * P].rearrange("p (j c) -> p j c", j=GT)
        wT = xt[:, :, :].rearrange("p k c -> p (k c)").rearrange("p (j c) -> p j c", j=GT)
        dbu = [dbu2[:, 0, :], dbu2[:, 1, :], yt[:, :, :].rearrange("p k c -> p (k c)")]
        free = GT * NT * P
        decay = [wxp_sb.rearrange("p k e -> p (k e)"), wdt_sb, hT[:, free:free + GW], decay_own]
        assert len(decay) == ASL == ND and free + GW == KH * P and ND * P == DI == GW
        assert GT * NT * P == 2 * C == GW and len(dbu) == NR and GT == 4
        projT = xt[:, :, :].rearrange("p k c -> p (k c)")
        xn4 = hact[:, :].rearrange("p (j c) -> p j c", c=C)
        xnT = hT[:, :].rearrange("p (c t) -> p c t", t=GW)
        assert GT * KC * P == H
        at[0] = 0
        w1_sb = carve(E, KC, H)
        w2_sb = carve(E, KH, C)
        assert KC * H == KH * C == ND * GW and E == 2 * NG
        b1_bc = carve(E, H)
        b2_bc = h_res[:, 0:E, :]
        W2_EARLY = 2
        at[0] = E * KC * H + W2_EARLY * KH * C
        hot_b = carve(TOPK * SEQS, P)
        to_add = carve(TOPK * SEQS, 3, TILES)
        top8 = carve(SEQS, 8)
        idx8 = carve(SEQS, 8).bitcast(U32)
        ex = carve(SEQS, E)
        ssum = carve(SEQS)
        rsum = carve(SEQS)
        pk = carve(TOPK, SEQS)
        pden = carve(SEQS)
        gate = carve(TOPK, SEQS)
        idx_f = carve(TOPK, SEQS)
        oh = carve(TOPK, SEQS, E)
        hot = carve(SEQS, E)
        cnt_et = carve(E, SEQS)
        inc_et = carve(E, SEQS)
        seg = carve(E, SEQS)
        place = carve(SEQS, E)
        cmp_k = carve(E, SEQS)
        nt_e = carve(E)
        cum_e = carve(E)
        off_e = carve(E)
        cmp_t = carve(TILES, E)
        tile_f = carve(TILES)
        slot_f = carve(TOPK, SEQS)
        slot_i = carve(TOPK, SEQS).bitcast(I32)
        slot_a = carve(TOPK, SEQS).bitcast(I32)
        slot_b = carve(TOPK, SEQS).bitcast(I32)
        a_f = carve(TOPK, SEQS)
        b_f = carve(TOPK, SEQS)
        unused = carve(TILES)
        picked = carve(TOPK, SEQS, E)

        y_ps, dbt_ps, b_ps, o_ps = psum[0:ND], psum[4:4 + NT], psum[5:7], psum[7]
        rank_ps, count_ps, order_ps = psum[3], psum[4], psum[5]
        up_ps, turn_ps, xturn_ps, down_ps = psum[0:2], psum[2:4], psum[6], psum[7]

        names = """ids_in weights_in setup_done ids_clean rows_clear a_bounded a_exp a_neg var1_ready rstd1_ready
            var2_ready rstd2_ready xn_ready xnT_ready in_ready step_ready conv_started conv_done
            xconv_ready zgate_ready proj_ready c_stored step_read step_logged dt_ready dt2_ready
            split_ready c_kept b_turned bT_ready dtu_turned dtuT_ready wT_ready wT_used dbt_ready
            pool_turns dve_turns act_turns dtu_ready decay_ready b_ready dbu_ready scan_ready g_ready
            g_used y_ready y_read yg_ready mix_ready h2_ready var3_ready rstd3_ready x2_ready x2_stored
            h2_stored x2_turned x2T_ready logits_ready logits_read mixer_done shifted expo_ready hot_ready
            ranks_ready order_ready onehots_ready lists_ready warmed bias_in experts_ready from_ready
            xt_turned xT_ready up_ready biased hact_ready hid_turned hT0_ready hT1_ready down_ready
            yt_ready to_ready yt_added yt_free out_stored zero_stored dve_chain act_chain pool_chain""".split()
        s = {n: sem(n) for n in names}
        emb_in = [sem(f"emb_in{g}") for g in range(3)]
        c_in = [sem(f"c_in{k}") for k in range(CSL)]
        e_in = [sem(f"expert_in{e}") for e in range(E)]
        x_in = [sem(f"xt_in{k}") for k in range(2)]

        def bc(ap, axis, *shape):
            return ap.unsqueeze(axis).broadcast_to([P, *shape])

        def seqs(ap):
            return ap.rearrange("p (s t) -> p s t", t=L)

        MIX0, MIX1, TURN0, TURN1, TURN2 = 2, 4, 8, 10, 12

        x_ps, turned_ps, proj_ps = psum[0:ND], psum[ND:ND + KC], psum[ND - 1]
        step_ps = z_ps = [psum[7], psum[4], psum[5], psum[6]]
        bturn_ps = psum[6]
        X_AT, Z_AT, IN, STEP = KC, KC + ND, KC + 2 * ND, 1 + ND

        block = ctx.enter_context(nc.Block())

        @block.sync
        def _(sp):
            sp.dma_start(id_raw[:, :], ids).then_inc(s["ids_in"], 16)
            loads = [
                (lnw_sb, ln_w.rearrange("(k p) -> p k", p=P)), (lnb_sb, ln_b.rearrange("(k p) -> p k", p=P)),
                (win_sb, w_in.rearrange("(k p) e -> p k e", p=P)),
                (convw_sb, conv_w.rearrange("(k p) t -> p k t", p=P)),
                (convb_sb, conv_b.rearrange("(k p) -> p k", p=P)),
                (wxp_sb[:, :, 0:PR], w_xp.rearrange("(k p) e -> p k e", p=P)),
                (wxp_sb[:, :, HALF:HALF + PR], w_xp.rearrange("(k p) e -> p k e", p=P)), (wdt_sb[0:R, :], w_dt),
                (bdt_sb, b_dt.rearrange("(k p) -> p k", p=P)),
                (a_sb, a_log.rearrange("(k p) n -> p k n", p=P)),
                (dskip_sb, d_skip.rearrange("(k p) -> p k", p=P)),
                (wout_sb, w_out.rearrange("(k p) c -> p k c", p=P)),
                (router_sb[:, :, :], w_router.rearrange("(k p) e -> p k e", p=P)),
            ]
            assert len(loads) == LOADS
            for dst, src in loads:
                sp.dma_start(dst, src, allow_slow_non_contiguous=True).then_inc(s["weights_in"], 16)
            sp.wait_ge(s["setup_done"], 1)
            sp.dma_start(sum_dram[NTOK:NTOK + P, :], zero_row[:, :]).then_inc(s["zero_stored"], 16)
            sp.sem_inc(s["c_kept"], 1)
            with sp.Fori(0, NG) as g:
                sp.wait_ge(s["proj_ready"], g + 1)
                sp.dma_start(c_dram[bass.ts(g, NS), :], projT[R + NS:PR, :]).then_inc(s["c_stored"], 16)
                sp.wait_ge(s["c_stored"], g * 16 + 16)
                sp.sem_inc(s["c_kept"], 1)
            sp.wait_ge(s["c_stored"], 16 * NG)
            sp.wait_ge(s["dt_ready"], 1 + NG * ND // 2)
            sp.wait_ge(s["dt2_ready"], 1 + NG * ND // 2)

            def load_c(q, k):
                sp.dma_start(c_bc[:, k, :], c_dram[bass.ds(q, 1), :].broadcast_to([P, GW])).then_inc(c_in[k], 16)

            for k in range(CSL):
                load_c(k, k)

            def next_c(m, k):
                q = m * CSL + k
                sp.wait_ge(s["g_ready"], ND + ND * (q - CSL + 1))
                load_c(q, k)

            def load_w1(e):
                sp.dma_start(w1_sb[:, e, :, :], w1[e].rearrange("(k p) h -> p k h", p=P)).then_inc(e_in[e], 16)

            def load_w2(e):
                sp.dma_start(w2_sb[:, e, :, :], w2[e].rearrange("(k p) c -> p k c", p=P)).then_inc(e_in[e], 16)

            MG = NS // CSL
            with sp.Fori(1, (NG - 1) * MG + 1) as m:
                for k in range(CSL):
                    next_c(m, k)
            early = []
            for e in range(NG - 1):
                early.append((load_w1, e))
                if e < W2_EARLY:
                    early.append((load_w2, e))
            early += [(load_w1, NG + e) for e in range(NG - 1)]
            sp.wait_ge(s["yg_ready"], 1 + ND * (NG - 1))
            for m in range((NG - 1) * MG + 1, NG * MG):
                for k in range(CSL):
                    next_c(m, k)
                    if early:
                        load, e = early.pop(0)
                        load(e)
            assert not early

            sp.wait_ge(s["mixer_done"], 1)
            sp.wait_ge(s["h2_stored"], 16 * NG)
            sp.wait_ge(s["x2_stored"], 16 * NG)
            sp.dma_start(b1_bc.rearrange("p e h -> p (e h)"),
                         b1.rearrange("(a e) h -> a (e h)", a=1).broadcast_to([P, E * H])).then_inc(s["bias_in"], 16)
            sp.dma_start(b2_bc.rearrange("p e c -> p (e c)"),
                         b2.rearrange("(a e) c -> a (e c)", a=1).broadcast_to([P, E * C])).then_inc(s["bias_in"], 16)
            load_w1(NG - 1)
            load_w1(2 * NG - 1)
            sp.wait_ge(s["lists_ready"], 1)
            for k in range(2):
                sp.wait_ge(x_in[k], 16)
            for e in range(E):
                if e >= W2_EARLY:
                    load_w2(e)
                sp.wait_ge(e_in[e], 32)
                sp.sem_inc(s["experts_ready"], 1)
            sp.wait_ge(s["yt_added"], 16 * TILES)
            sp.dma_start(out.rearrange("s t c -> (s t) c"), sum_dram[0:NTOK, :]).then_inc(s["out_stored"], 16)
            sp.wait_ge(s["out_stored"], 16)

        @block.gpsimd
        def _(pool):
            chain = Chain(pool, s["pool_chain"])
            pool.sem_inc(s["yt_free"], 2)
            pool.sem_inc(s["dt_ready"], 1)
            nc.gpsimd.memset(zero_row[:, :], 0.0).then_inc(s["setup_done"], 1)
            chain.then(nc.gpsimd.memset(ident[:, :], 0.0))
            chain.then(nc.gpsimd.memset(before[:, :], 1.0))
            chain.then(nc.gpsimd.memset(ones[:, :], 1.0))
            chain.then(nc.gpsimd.memset(power[:, :], -0.5))
            rows = [(iota_p, [[1, P]], 0, 0), (iota_k, [[P, SEQS]], 0, 0), (iota_t, [[1, TILES]], 0, 0),
                    (token, [[L, SEQS]], 0, 1), (spare, [[0, 1]], NTOK, 1)]
            for dst, pattern, base, per_partition in rows:
                chain.then(nc.gpsimd.iota(dst[:, :], pattern, base, per_partition,
                                          allow_small_or_imprecise_dtypes=True))
            chain.settle()
            nc.gpsimd.affine_select(out=ident[:, :], in_=ident[:, :], compare_op=ALU.not_equal, fill=1.0,
                                    base=0, pattern=[[-1, P]], channel_multiplier=1).then_inc(s["setup_done"], 1)
            nc.gpsimd.affine_select(out=before[:, :], in_=before[:, :], compare_op=ALU.is_gt, fill=0.0,
                                    base=0, pattern=[[1, P]], channel_multiplier=-1).then_inc(s["setup_done"], 1)
            pool.wait_ge(s["ids_clean"], 1)

            def gather(g):
                for i in range(g * GT, g * GT + GT):
                    nc.gpsimd.indirect_dma_start(
                        out=h_res[:, i, :], out_offset=None, in_=emb_w,
                        in_offset=bass.IndirectOffsetOnAxis(ap=id_u[:, i:i + 1], axis=0)).then_inc(emb_in[min(g, 2)], 16)

            def inputs(g):
                pool.wait_ge(s["var1_ready"], g + 1)
                nc.gpsimd.tensor_tensor(rstdf[:, :], varf[:, :], power[:, 0:GT], ALU.pow).then_inc(s["rstd1_ready"], 1)
                pool.wait_ge(s["var2_ready"], g + 1)
                nc.gpsimd.tensor_tensor(rstdg[:, :], varg[:, :], power[:, 0:GT], ALU.pow).then_inc(s["rstd2_ready"], 1)

            def past():
                pool.sem_inc(s["pool_turns"], 1)

            def steps(g):
                for d in range(ND // 2):
                    k = d
                    pool.wait_ge(s["step_logged"], g * ND + d + 1)
                    past()
                    chain.then(nc.gpsimd.tensor_scalar(sp_t[:, k, :], sp_e[:, d, :], 1.0, -1.0, ALU.add, ALU.add))
                    chain.settle()
                    past()
                    chain.then(nc.gpsimd.tensor_tensor(sp_t[:, k, :], sp_e[:, d, :], sp_t[:, k, :], ALU.subtract))
                    chain.settle()
                    past()
                    chain.then(nc.gpsimd.tensor_tensor(sp_t[:, k, :], sp_t[:, k, :], dt_sb[:, g, d, :], ALU.add))
                    chain.settle()
                    past()
                    nc.gpsimd.tensor_tensor(dt_sb[:, g, d, :], sp_t[:, k, :], sp_r[:, d, :],
                                            ALU.add).then_inc(s["dt_ready"], 1)

            gather(0)
            gather(1)
            inputs(0)
            inputs(1)
            for g in range(2, NG):
                gather(g)
            with pool.Fori(0, NG - 2) as g:
                chain.enter(g, 3 * ND // 2)
                inputs(g + 2)
                steps(g)
                chain.leave(NG - 2)
            steps(NG - 2)
            steps(NG - 1)

            pool.sem_inc(s["g_ready"], ND)

            def products(m):
                for k in range(CSL):
                    for d in range(ND):
                        u = (m * CSL + k) * ND + d
                        if d == 0:
                            pool.wait_ge(c_in[k], 16 * m + 16)
                        pool.wait_ge(s["scan_ready"], ASL + u + 1)
                        pool.wait_ge(s["g_used"], u + 1)
                        nc.gpsimd.tensor_tensor(g_buf[:, d, :], h_buf[:, d, :], c_bc[:, k, :],
                                                ALU.mult).then_inc(s["g_ready"], 1)

            def root(g):
                pool.wait_ge(s["var3_ready"], g + 1)
                nc.gpsimd.tensor_tensor(rstdh[:, :], varh[:, :], power[:, 0:GT], ALU.pow).then_inc(s["rstd3_ready"], 1)

            MG = NS // CSL
            with pool.Fori(0, MG) as m:
                products(m)
            with pool.Fori(1, NG) as g:
                products(g * MG)
                products(g * MG + 1)
                root(g - 1)
                with pool.Fori(2, MG) as m:
                    products(g * MG + m)
            root(NG - 1)

            def load_x(i, k, turned=True):
                pool.wait_ge(s["from_ready"], i + 1)
                if turned:
                    pool.wait_ge(s["xt_turned"], i - 1)
                past()
                nc.gpsimd.indirect_dma_start(
                    out=xt[:, k, :], out_offset=None, in_=x2_dram,
                    in_offset=bass.IndirectOffsetOnAxis(ap=from_u[k][:, :], axis=0)).then_inc(x_in[k], 16)

            def add_y(i, k, first=False):
                pool.wait_ge(s["to_ready"], i + 1)
                pool.wait_ge(s["yt_ready"], i + 2)
                if not first:
                    pool.wait_ge(s["yt_added"], 16 * i)
                    pool.sem_inc(s["yt_free"], 1)
                past()
                nc.gpsimd.indirect_dma_start(
                    out=sum_dram, out_offset=bass.IndirectOffsetOnAxis(ap=to_u[k][:, :], axis=0),
                    in_=yt[:, k, :], in_offset=None, compute_op=ALU.add).then_inc(s["yt_added"], 16)

            pool.wait_ge(s["x2_stored"], 16 * NG)
            load_x(0, 0, False)
            load_x(1, 1, False)
            load_x(2, 0)
            pool.wait_ge(s["h2_stored"], 16 * NG)
            pool.wait_ge(s["zero_stored"], 16)
            load_x(3, 1)
            add_y(0, 0, True)
            with pool.Fori(0, (TILES - 5) // 2) as m:
                for k in range(2):
                    load_x(2 * m + k + 4, k)
                    add_y(2 * m + k + 1, 1 - k)
            for i in range(TILES - 4, TILES):
                if i + 3 < TILES:
                    load_x(i + 3, (i + 3) % 2)
                add_y(i, i % 2)

        @block.scalar
        def _(act):
            chain = Chain(act, s["act_chain"])
            for ahead in ("logits_read", "xconv_ready", "step_read", "hT0_ready", "xT_ready"):
                act.sem_inc(s[ahead], 1)
            act.wait_ge(s["a_bounded"], 1)
            nc.scalar.activation(a_sb, a_sb, ACT.Exp).then_inc(s["a_exp"], 1)
            act.wait_ge(s["weights_in"], 16 * LOADS)

            def past():
                act.sem_inc(s["act_turns"], 1)

            def store_post(g):
                act.wait_ge(s["h2_ready"], g * GT + GT)
                act.dma_start(sum_dram[bass.ts(g, GW), :].rearrange("(j p) c -> p j c", p=P),
                              h_res[:, bass.ts(g, GT), :]).then_inc(s["h2_stored"], 16)
                act.wait_ge(s["x2_ready"], g * GT + GT)
                act.dma_start(x2_dram[bass.ts(g, GW), :].rearrange("(j p) c -> p j c", p=P),
                              x2).then_inc(s["x2_stored"], 16)

            def turned(g):
                for c in range(KC):
                    act.wait_ge(s["in_ready"], g * IN + c + 1)
                    nc.scalar.activation(xnT[:, c, :], turned_ps[c][:, :], ACT.Identity,
                                         bias=lnb_sb[:, c:c + 1], scale=lnw_sb[:, c:c + 1]).then_inc(s["xnT_ready"], 1)

            def conv_starts(g):
                for d in range(ND):
                    if not (isinstance(g, int) and g == 0):
                        act.wait_ge(s["xconv_ready"], 1 + (g - 1) * ND + d + 1)
                    act.wait_ge(s["in_ready"], g * IN + X_AT + d + 1)
                    nc.scalar.activation(conv_acc[:, d, :], x_ps[d][:, :], ACT.Identity,
                                         bias=convb_sb[:, d:d + 1],
                                         scale=convw_sb[:, d, TAPS - 1:TAPS]).then_inc(s["conv_started"], 1)

            def conv_outs(g):
                for d in range(ND):
                    act.wait_ge(s["conv_done"], g * ND + d + 1)
                    nc.scalar.activation(xconv[:, g, d, :], conv_acc[:, d, :],
                                         ACT.Silu).then_inc(s["xconv_ready"], 1)

            def gates(g):
                for d in range(ND):
                    act.wait_ge(s["in_ready"], g * IN + Z_AT + d + 1)
                    nc.scalar.activation(zgate[:, g, d, :], z_ps[d][:, :],
                                         ACT.Silu).then_inc(s["zgate_ready"], 1)

            def projected(g):
                act.wait_ge(s["step_ready"], g * STEP + 1)
                act.wait_ge(s["split_ready"], 1 + 2 * g)
                act.wait_ge(s["c_kept"], 1 + g)
                nc.scalar.activation(projT, proj_ps[:, :], ACT.Copy).then_inc(s["proj_ready"], 1)

            def step_inputs(g):
                act.wait_ge(s["dt_ready"], 1 + g * (ND // 2))
                act.wait_ge(s["dt2_ready"], 1 + g * (ND // 2))
                act.wait_ge(s["b_turned"], g + 1)
                past()
                nc.scalar.activation(bT[:, :, bass.ts(g, NS)],
                                     bturn_ps[:, :].rearrange("p (j r) -> p j r", r=P)[:, :, R:R + NS],
                                     ACT.Copy).then_inc(s["bT_ready"], 1)
                for d in range(ND):
                    act.wait_ge(s["step_ready"], g * STEP + d + 2)
                    chain.then(nc.scalar.activation(sp_e[:, d, :], step_ps[d][:, :], ACT.Abs,
                                                    bias=bdt_sb[:, d:d + 1]))
                    nc.scalar.activation(sp_r[:, d, :], step_ps[d][:, :], ACT.Relu,
                                         bias=bdt_sb[:, d:d + 1]).then_inc(s["step_read"], 1)

            def steps(g):
                chain.settle()
                chain.then(nc.scalar.activation(sp_e, sp_e, ACT.Exp, scale=-1.0))
                chain.settle()
                for d in range(ND):
                    nc.scalar.activation(dt_sb[:, g, d, :], sp_e[:, d, :], ACT.Ln,
                                         bias=1.0).then_inc(s["step_logged"], 1)

            turned(0)
            conv_starts(0)
            conv_outs(0)
            gates(0)
            with act.Fori(1, NG) as g:
                chain.enter(g - 1, ND + 1)
                turned(g)
                projected(g - 1)
                conv_starts(g)
                step_inputs(g - 1)
                conv_outs(g)
                steps(g - 1)
                gates(g)
                chain.leave(NG - 1)
            projected(NG - 1)
            step_inputs(NG - 1)
            steps(NG - 1)

            act.wait_ge(s["a_neg"], 1)
            nc.scalar.activation(warm[:, :], a_sb[:, 0, 0:1], ACT.Exp).then_inc(s["warmed"], 1)
            act.wait_ge(s["dt_ready"], 1 + NG * ND // 2)
            act.wait_ge(s["dt2_ready"], 1 + NG * ND // 2)
            act.wait_ge(s["bT_ready"], NG)
            act.wait_ge(s["c_kept"], 1 + NG)
            act.wait_ge(s["split_ready"], 1 + 2 * NG)

            def inputs_turned(g):
                for b in range(NT):
                    act.wait_ge(s["dtu_turned"], g * NT + b + 1)
                    nc.scalar.activation(dtuT[:, :, bass.ts(b, P)],
                                         dbt_ps[b][:, :].rearrange("p (j c) -> p j c", j=GT),
                                         ACT.Copy).then_inc(s["dtuT_ready"], 1)

            def with_b(q, half):
                if half == 0:
                    act.wait_ge(s["wT_used"], 1 + q)
                for j in range(2):
                    nc.scalar.activation(wT[:, 2 * half + j, :], dtuT[:, 2 * half + j, :], ACT.Copy,
                                         scale=bT[:, 2 * half + j, bass.ds(q, 1)]).then_inc(s["wT_ready"], 1)

            def decay_of(g, n, d):
                act.wait_ge(s["scan_ready"], (g * NS + n) * ND + d + 1)
                if isinstance(n, int):
                    past()
                nc.scalar.activation(seqs(decay[d])[:, :, 1:L], seqs(dt_sb[:, g, d, :])[:, :, 1:L],
                                     ACT.Exp, scale=a_sb[:, d, bass.ds(n, 1)]).then_inc(s["decay_ready"], 1)

            def first_decays(g):
                decay_of(g, 0, 0)
                decay_of(g, 0, 1)
                inputs_turned(g)
                act.wait_ge(s["dtuT_ready"], g * NT + NT)
                with_b(g * NS, 0)
                with_b(g * NS, 1)
                decay_of(g, 0, 2)
                decay_of(g, 0, 3)

            def decays(g, n0, n1):
                with act.Fori(n0, n1) as n:
                    for d in range(ND):
                        if d < 2:
                            with_b(g * NS + n, d)
                        decay_of(g, n, d)

            def x2T_copy(g, half):
                act.wait_ge(s["x2_turned"], 2 * g + half + 1)
                nc.scalar.activation(x2T[:, bass.ts(half, BANK)], o_ps[:, :], ACT.Copy).then_inc(s["x2T_ready"], 1)

            def logits_copy(g):
                act.wait_ge(s["logits_ready"], g + 1)
                past()
                nc.scalar.activation(lg[:, bass.ts(g, GT), :], o_ps[:, 0:GT * E].rearrange("p (i e) -> p i e", e=E),
                                     ACT.Copy).then_inc(s["logits_read"], 1)

            first_decays(0)
            decays(0, 1, NS)
            with act.Fori(1, NG) as g:
                first_decays(g)
                decays(g, 1, TURN0 + 2)
                store_post(g - 1)
                x2T_copy(g - 1, 0)
                decays(g, TURN0 + 2, TURN1 + 2)
                x2T_copy(g - 1, 1)
                decays(g, TURN1 + 2, NS - 1)
                logits_copy(g - 1)
                decays(g, NS - 1, NS)
            store_post(NG - 1)
            x2T_copy(NG - 1, 0)
            x2T_copy(NG - 1, 1)
            logits_copy(NG - 1)

            act.wait_ge(s["shifted"], 1)
            nc.scalar.activation(ex, ex, ACT.Exp).then_inc(s["expo_ready"], 1)

            def xT_copy(i):
                act.wait_ge(s["xt_turned"], i + 1)
                nc.scalar.activation(xT[:, :], xturn_ps[:, 0:KC * P], ACT.Copy).then_inc(s["xT_ready"], 1)

            def gelu(i):
                for b in range(HB):
                    act.wait_ge(s["biased"], HB * i + b + 1)
                    nc.scalar.activation(hact[:, bass.ts(b, BANK)], up_ps[b][:, :],
                                         ACT.Gelu_apprx_tanh).then_inc(s["hact_ready"], 1)

            def hT_copy(i):
                act.wait_ge(s["hid_turned"], 2 * i + 1)
                nc.scalar.activation(hT[:, 0:BANK], turn_ps[0][:, :], ACT.Copy).then_inc(s["hT0_ready"], 1)

            xT_copy(0)
            gelu(0)
            xT_copy(1)
            with act.Fori(0, TILES - 2) as i:
                hT_copy(i)
                gelu(i + 1)
                xT_copy(i + 2)
            hT_copy(TILES - 2)
            gelu(TILES - 1)
            hT_copy(TILES - 1)

        @block.vector
        def _(dve):
            chain = Chain(dve, s["dve_chain"])
            for ahead in ("dbu_ready", "yg_ready", "hT1_ready", "yt_ready", "dt2_ready",
                          "split_ready"):
                dve.sem_inc(s[ahead], 1)
            dve.wait_ge(s["ids_in"], 16)
            chain.then(nc.vector.tensor_copy(id_f[:, :], id_raw[:, :]))
            chain.settle()
            chain.then(nc.vector.tensor_scalar(id_c[:, :], id_f[:, :], 0.0, float(VOCAB - 1), ALU.max, ALU.min))
            chain.settle()
            nc.vector.tensor_copy(id_u[:, :], id_c[:, :]).then_inc(s["ids_clean"], 1)
            chain.then(nc.vector.tensor_tensor(id_ok[:, :], id_c[:, :], id_f[:, :], ALU.is_equal))
            for at_row in (0, HALF):
                nc.vector.memset(wxp_sb[:, :, at_row + PR:at_row + HALF], 0.0).then_inc(s["rows_clear"], 1)
            dve.wait_ge(s["setup_done"], 3)
            nc.vector.tensor_tensor(pick_b[:, :], ident[:, R:R + NS], ident[:, HALF + R:HALF + R + NS],
                                    ALU.add).then_inc(s["rows_clear"], 1)
            dve.wait_ge(s["weights_in"], 16 * LOADS)
            nc.vector.tensor_scalar(a_sb, a_sb, A_LOG_MAX, None, ALU.min).then_inc(s["a_bounded"], 1)
            chain.settle()
            dve.wait_ge(s["a_exp"], 1)
            nc.vector.tensor_scalar(a_sb, a_sb, -1.0, None, ALU.mult).then_inc(s["a_neg"], 1)

            def first_norm(dst, i):
                return nc.vector.tensor_scalar(dst, h_res[:, bass.ds(i, 1), :], mean1[:, bass.ds(i, 1)],
                                               rstd1[:, bass.ds(i, 1)], ALU.subtract, ALU.mult)

            def past():
                dve.sem_inc(s["dve_turns"], 1)

            def variances(g, mv, var, ready):
                past()
                for j in range(GT):
                    chain.then(nc.vector.bn_aggr(mv[:, j, :], st[:, j, :]))
                chain.settle()
                nc.vector.tensor_scalar(var[:, :], mv[:, :, 1], EPS, None, ALU.add).then_inc(s[ready], 1)

            def first_norms(g):
                if not (isinstance(g, int) and g == 0):
                    dve.wait_ge(s["xn_ready"], g * GT)
                for j in range(GT):
                    i = g * GT + j
                    chain.then(nc.vector.tensor_scalar(h_res[:, bass.ds(i, 1), :], h_res[:, bass.ds(i, 1), :],
                                                       id_ok[:, bass.ds(i, 1)], None, ALU.mult))
                chain.settle()
                past()
                for j in range(GT):
                    chain.then(nc.vector.bn_stats(st[:, j, :], h_res[:, bass.ds(g * GT + j, 1), :]))
                chain.settle()
                variances(g, mvf, varf, "var1_ready")
                dve.wait_ge(s["rstd1_ready"], g + 1)
                for j in range(GT):
                    chain.then(nc.vector.tensor_scalar(x1[:, j, :], h_res[:, bass.ds(g * GT + j, 1), :], mvf[:, j, 0:1],
                                                       rstdf[:, j:j + 1], ALU.subtract, ALU.mult))
                chain.then(nc.vector.tensor_scalar(mean1[:, bass.ts(g, GT)], mvf[:, :, 0], 1.0, None, ALU.mult))
                chain.then(nc.vector.tensor_scalar(rstd1[:, bass.ts(g, GT)], rstdf[:, :], 1.0, None, ALU.mult))
                chain.settle()
                past()
                for j in range(GT):
                    chain.then(nc.vector.bn_stats(st[:, j, :], x1[:, j, :]))
                chain.settle()
                variances(g, mvg, varg, "var2_ready")

            def second_norms(g):
                if not (isinstance(g, int) and g == 0):
                    dve.wait_ge(s["in_ready"], (g - 1) * IN + KC)
                dve.wait_ge(s["rstd2_ready"], g + 1)
                for j in range(GT):
                    nc.vector.tensor_scalar(xn4[:, j, :], x1[:, j, :], mvg[:, j, 0:1], rstdg[:, j:j + 1],
                                            ALU.subtract, ALU.mult).then_inc(s["xn_ready"], 1)

            def convs(g):
                for back in range(1, TAPS):
                    for d in range(ND):
                        if back == 1:
                            dve.wait_ge(s["conv_started"], g * ND + d + 1)
                        x, acc = seqs(x_ps[d][:, :]), seqs(conv_acc[:, d, :])
                        ins = nc.vector.scalar_tensor_tensor(
                            out=acc[:, :, back:L], in0=x[:, :, 0:L - back],
                            scalar=convw_sb[:, d, TAPS - 1 - back:TAPS - back], in1=acc[:, :, back:L],
                            op0=ALU.mult, op1=ALU.add)
                        if back < TAPS - 1:
                            chain.then(ins)
                        else:
                            ins.then_inc(s["conv_done"], 1)
                    if back < TAPS - 1:
                        chain.settle()

            def split(g):
                dve.wait_ge(s["proj_ready"], g + 1)
                dve.wait_ge(s["split_ready"], 1 + 2 * g)
                past()
                chain.then(nc.vector.tensor_scalar(proj_hi.bitcast(I32), projT.bitcast(I32), HIGH, None,
                                                   ALU.bitwise_and))
                chain.settle()
                past()
                nc.vector.tensor_scalar(proj_hl[0:HALF, g, :], proj_hi[0:HALF, :], 1.0, None,
                                        ALU.mult).then_inc(s["split_ready"], 1)
                nc.vector.tensor_tensor(proj_hl[HALF:P, g, :], projT[HALF:P, :], proj_hi[HALF:P, :],
                                        ALU.subtract).then_inc(s["split_ready"], 1)

            def steps(g):
                for d in range(ND // 2, ND):
                    dve.wait_ge(s["step_logged"], g * ND + d + 1)
                    chain.then(nc.vector.tensor_scalar(sp_t[:, d, :], sp_e[:, d, :], 1.0, -1.0, ALU.add, ALU.add))
                chain.settle()
                for d in range(ND // 2, ND):
                    chain.then(nc.vector.tensor_tensor(sp_t[:, d, :], sp_e[:, d, :], sp_t[:, d, :], ALU.subtract))
                chain.settle()
                for d in range(ND // 2, ND):
                    chain.then(nc.vector.tensor_tensor(sp_t[:, d, :], sp_t[:, d, :], dt_sb[:, g, d, :], ALU.add))
                chain.settle()
                for d in range(ND // 2, ND):
                    nc.vector.tensor_tensor(dt_sb[:, g, d, :], sp_t[:, d, :], sp_r[:, d, :],
                                            ALU.add).then_inc(s["dt2_ready"], 1)

            dve.wait_ge(emb_in[0], 16 * GT)
            first_norms(0)
            second_norms(0)
            dve.wait_ge(emb_in[1], 16 * GT)
            first_norms(1)
            second_norms(1)
            convs(0)
            dve.wait_ge(emb_in[2], 16 * GT * (NG - 2))
            with dve.Fori(1, NG - 1) as g:
                chain.enter(g - 1, 6 * GT + 2 + (TAPS - 2) * ND + 1 + 3 * ND // 2)
                split(g - 1)
                convs(g)
                first_norms(g + 1)
                second_norms(g + 1)
                steps(g - 1)
                chain.leave(NG - 2)
            split(NG - 2)
            convs(NG - 1)
            steps(NG - 2)
            split(NG - 1)
            steps(NG - 1)

            dve.wait_ge(s["dt_ready"], 1 + NG * ND // 2)
            dve.wait_ge(s["dt2_ready"], 1 + NG * ND // 2)
            for k in range(ASL):
                nc.vector.memset(seqs(decay[k])[:, :, 0:1], 0.0).then_inc(s["scan_ready"], 1)

            def inputs(g, turned):
                if turned and not (isinstance(g, int) and g == 0):
                    dve.wait_ge(s["dtu_turned"], g * NT)
                for d in range(NR, ND) if turned else range(NR):
                    nc.vector.tensor_tensor(dtu[:, d, :], dt_sb[:, g, d, :], xconv[:, g, d, :],
                                            ALU.mult).then_inc(s["dtu_ready"], 1)

            def step(g, n, between=None, odd=None):
                if odd is None:
                    odd = n % 2
                q = g * NS + n

                def input_of(d):
                    if d == 0:
                        dve.wait_ge(s["dtu_ready"], g * ND + ND)
                        dve.wait_ge(s["b_ready"], q + 1)
                    dve.wait_ge(s["scan_ready"], ASL + (q - 1) * ND + d + 1)
                    nc.vector.tensor_tensor(dbu[d], dtu[:, d, :], b_ps[odd][:, :], ALU.mult
                                            ).then_inc(s["dbu_ready"], 1)

                def scan_of(d):
                    u = q * ND + d
                    dve.wait_ge(s["decay_ready"], u + 1)
                    if d < NR:
                        dve.wait_ge(s["dbu_ready"], 1 + q * NR + d + 1)
                    else:
                        dve.wait_ge(s["dbt_ready"], q * NT + d - NR + 1)
                    dve.wait_ge(s["g_ready"], u + 1)
                    source = dbu[d] if d < NR else dbt_ps[d - NR][:, :]
                    nc.vector.tensor_tensor_scan(h_buf[:, d, :], decay[d], source, 0.0,
                                                 ALU.mult, ALU.add).then_inc(s["scan_ready"], 1)

                input_of(0)
                input_of(1)
                for d in range(ND):
                    if d == 2 and between:
                        between()
                    scan_of(d)
                    if d + 2 < NR:
                        input_of(d + 2)

            def with_skip(g):
                for d in range(ND):
                    dve.wait_ge(s["y_ready"], g * ND + d + 1)
                    nc.vector.scalar_tensor_tensor(
                        out=yg[:, d, :], in0=xconv[:, g, d, :], scalar=dskip_sb[:, d:d + 1], in1=y_ps[d][:, :],
                        op0=ALU.mult, op1=ALU.add).then_inc(s["y_read"], 1)

            def gated(g, half):
                for d in (2 * half, 2 * half + 1):
                    dve.wait_ge(s["y_read"], g * ND + d + 1)
                    nc.vector.tensor_tensor(yg[:, d, :], yg[:, d, :], zgate[:, g, d, :],
                                            ALU.mult).then_inc(s["yg_ready"], 1)

            def residual(g, half):
                for j in (2 * half, 2 * half + 1):
                    chain.then(first_norm(x1tmp[:, j % 2, :], g * GT + j))
                chain.settle()
                for j in (2 * half, 2 * half + 1):
                    i = g * GT + j
                    chain.then(nc.vector.tensor_tensor(h_res[:, bass.ds(i, 1), :], h_res[:, bass.ds(i, 1), :],
                                                       x1tmp[:, j % 2:j % 2 + 1, :], ALU.add))

            def mixed(g, half):
                chain.settle()
                dve.wait_ge(s["mix_ready"], 2 * g + half + 1)
                for j in (2 * half, 2 * half + 1):
                    i = g * GT + j
                    nc.vector.tensor_tensor(h_res[:, bass.ds(i, 1), :], h_res[:, bass.ds(i, 1), :],
                                            o_ps[:, bass.ts(j % 2, C)].unsqueeze(1), ALU.add
                                            ).then_inc(s["h2_ready"], 1)
                dve.wait_ge(s["h2_ready"], g * GT + 2 * half + 2)
                past()
                for j in (2 * half, 2 * half + 1):
                    chain.then(nc.vector.bn_stats(st[:, j, :], h_res[:, bass.ds(g * GT + j, 1), :]))
                chain.settle()

            def third_norm(g):
                if not (isinstance(g, int) and g == 0):
                    dve.wait_ge(s["x2_stored"], g * 16)
                    dve.wait_ge(s["x2_turned"], g * 2)
                dve.wait_ge(s["rstd3_ready"], g + 1)
                for j in range(GT):
                    nc.vector.tensor_scalar(x2[:, j, :], h_res[:, bass.ds(g * GT + j, 1), :], mvh[:, j, 0:1],
                                            rstdh[:, j:j + 1], ALU.subtract, ALU.mult).then_inc(s["x2_ready"], 1)

            inputs(0, True)
            inputs(0, False)
            with dve.Fori(0, NS // 2 - 1) as m:
                for odd in range(2):
                    step(0, 2 * m + odd, odd=odd)
            with dve.Fori(1, NG) as g:
                chain.enter(g - 1, 6 * 2 + GT)
                step(g - 1, NS - 2)
                inputs(g, True)
                step(g - 1, NS - 1)
                inputs(g, False)
                step(g, 0, lambda: with_skip(g - 1))
                step(g, 1)
                gated(g - 1, 0)
                step(g, 2)
                gated(g - 1, 1)
                step(g, 3)
                residual(g - 1, 0)
                step(g, 4)
                mixed(g - 1, 0)
                step(g, 5)
                residual(g - 1, 1)
                step(g, 6)
                mixed(g - 1, 1)
                step(g, 7)
                variances(g - 1, mvh, varh, "var3_ready")
                step(g, 8)
                third_norm(g - 1)
                step(g, 9)
                with dve.Fori(5, NS // 2 - 1) as m:
                    for odd in range(2):
                        step(g, 2 * m + odd, odd=odd)
                chain.leave(NG - 1)
            step(NG - 1, NS - 2)
            step(NG - 1, NS - 1)
            with_skip(NG - 1)
            for half in range(2):
                gated(NG - 1, half)
            for half in range(2):
                residual(NG - 1, half)
                mixed(NG - 1, half)
            dve.sem_inc(s["mixer_done"], 1)
            variances(NG - 1, mvh, varh, "var3_ready")
            third_norm(NG - 1)

            dve.wait_ge(s["logits_read"], 1 + NG)
            dve.wait_ge(s["x2_stored"], 16 * NG)
            for i in range(SEQS):
                chain.then(nc.vector.max(top8[:, i, :], lg[:, i, :]))
            chain.settle()
            nc.vector.tensor_tensor(ex, lg[:, :, :], top8[:, :, 0:1].broadcast_to([P, SEQS, E]),
                                    ALU.subtract).then_inc(s["shifted"], 1)
            for i in range(SEQS):
                chain.then(nc.vector.max_index(idx8[:, i, :], top8[:, i, :], lg[:, i, :]))
            chain.settle()
            for j in range(TOPK):
                chain.then(nc.vector.tensor_copy(idx_f[:, j, :], idx8[:, :, j]))
            chain.settle()
            for j in range(TOPK):
                chain.then(nc.vector.tensor_tensor(oh[:, j, :, :], bc(idx_f[:, j, :], 2, SEQS, E),
                                                   bc(iota_p[:, 0:E], 1, SEQS, E), ALU.is_equal))
            chain.settle()
            nc.vector.tensor_tensor(hot, oh[:, 0, :, :], oh[:, 1, :, :], ALU.add).then_inc(s["hot_ready"], 1)
            dve.wait_ge(s["expo_ready"], 1)
            chain.then(nc.vector.reduce_sum(ssum, ex, AX_X))
            for j in range(TOPK):
                chain.then(nc.vector.tensor_tensor(picked[:, j, :, :], oh[:, j, :, :], ex, ALU.mult))
            chain.settle()
            chain.then(nc.vector.reciprocal(rsum, ssum))
            for j in range(TOPK):
                chain.then(nc.vector.reduce_sum(pk[:, j, :], picked[:, j, :, :], AX_X))
            chain.settle()
            for j in range(TOPK):
                chain.then(nc.vector.tensor_tensor(pk[:, j, :], pk[:, j, :], rsum, ALU.mult))
            chain.settle()
            chain.then(nc.vector.tensor_tensor(pden, pk[:, 0, :], pk[:, 1, :], ALU.add))
            chain.settle()
            chain.then(nc.vector.tensor_scalar(pden, pden, 1e-8, None, ALU.add))
            chain.settle()
            chain.then(nc.vector.reciprocal(pden, pden))
            chain.settle()
            for j in range(TOPK):
                chain.then(nc.vector.tensor_tensor(gate[:, j, :], pk[:, j, :], pden, ALU.mult))

            dve.wait_ge(s["ranks_ready"], 1)
            chain.then(nc.vector.tensor_copy(cnt_et, count_ps[:, 0:SEQS * E].rearrange("p (i e) -> p e i", e=E)))
            chain.then(nc.vector.memset(seg, 1.0))
            chain.settle()
            chain.then(nc.vector.memset(seg[:, :, 0:1], 0.0))
            chain.settle()
            chain.then(nc.vector.tensor_tensor_scan(
                inc_et.rearrange("p e i -> p (e i)"), seg.rearrange("p e i -> p (e i)"),
                cnt_et.rearrange("p e i -> p (e i)"), 0.0, ALU.mult, ALU.add))
            chain.settle()
            chain.then(nc.vector.tensor_tensor(cmp_k, inc_et[:, :, SEQS - 1:SEQS].broadcast_to([P, E, SEQS]),
                                               bc(iota_k[:, :], 1, E, SEQS), ALU.is_gt))
            chain.settle()
            chain.then(nc.vector.reduce_sum(nt_e, cmp_k, AX_X))
            chain.settle()
            chain.then(nc.vector.tensor_tensor_scan(cum_e, ones[:, 0:E], nt_e, 0.0, ALU.mult, ALU.add))
            chain.settle()
            chain.then(nc.vector.tensor_tensor(off_e, cum_e, nt_e, ALU.subtract))
            chain.then(nc.vector.tensor_tensor(cmp_t, bc(cum_e, 1, TILES, E), bc(iota_t[:, :], 2, TILES, E), ALU.is_le))
            chain.settle()
            chain.then(nc.vector.tensor_scalar(off_e, off_e, float(P), None, ALU.mult))
            chain.then(nc.vector.reduce_sum(tile_f, cmp_t, AX_X))
            chain.settle()
            chain.then(nc.vector.tensor_scalar(tile_e[:, :], tile_f, float(E - 1), None, ALU.min))
            chain.then(nc.vector.tensor_tensor(inc_et, inc_et, cnt_et, ALU.subtract))
            chain.settle()
            chain.then(nc.vector.tensor_tensor(inc_et, inc_et, bc(off_e, 2, E, SEQS), ALU.add))
            chain.settle()
            chain.then(nc.vector.tensor_tensor(place, rank_ps[:, 0:SEQS * E].rearrange("p (i e) -> p i e", e=E),
                                               inc_et.rearrange("p e i -> p i e"), ALU.add))
            chain.settle()
            for j in range(TOPK):
                chain.then(nc.vector.tensor_tensor(picked[:, j, :, :], oh[:, j, :, :], place, ALU.mult))
            chain.settle()
            for j in range(TOPK):
                chain.then(nc.vector.reduce_sum(slot_f[:, j, :], picked[:, j, :, :], AX_X))
            chain.settle()
            chain.then(nc.vector.tensor_copy(slot_i, slot_f))
            chain.settle()
            chain.then(nc.vector.tensor_scalar(slot_a, slot_i, P.bit_length() - 1, None, ALU.arith_shift_right))
            chain.then(nc.vector.tensor_scalar(slot_b, slot_i, P - 1, None, ALU.bitwise_and))
            chain.settle()
            chain.then(nc.vector.tensor_copy(a_f, slot_a))
            chain.then(nc.vector.tensor_copy(b_f, slot_b))
            chain.settle()
            for j in range(TOPK):
                tiles_of = to_add[:, j * SEQS:(j + 1) * SEQS, :, :]
                chain.then(nc.vector.tensor_tensor(tiles_of[:, :, 2, :], bc(iota_t[:, :], 1, SEQS, TILES),
                                                   bc(a_f[:, j, :], 2, SEQS, TILES), ALU.is_equal))
                chain.settle()
                chain.then(nc.vector.tensor_tensor(tiles_of[:, :, 0, :], tiles_of[:, :, 2, :],
                                                   bc(token[:, :], 2, SEQS, TILES), ALU.mult))
                chain.then(nc.vector.tensor_tensor(tiles_of[:, :, 1, :], tiles_of[:, :, 2, :],
                                                   bc(gate[:, j, :], 2, SEQS, TILES), ALU.mult))
                chain.settle()
                for i in range(SEQS):
                    nc.vector.tensor_scalar(hot_b[:, j * SEQS + i, :], iota_p[:, :], b_f[:, j, i:i + 1], None,
                                            ALU.is_equal).then_inc(s["onehots_ready"], 1)
            dve.wait_ge(s["order_ready"], 1)
            chain.then(nc.vector.tensor_copy(from_t[:, :], order_ps[:, 0:TILES]))
            chain.then(nc.vector.tensor_copy(gate_t[:, :], order_ps[:, TILES:2 * TILES]))
            chain.then(nc.vector.tensor_scalar(unused, order_ps[:, 2 * TILES:3 * TILES], -1.0, 1.0, ALU.mult, ALU.add))
            chain.settle()
            chain.then(nc.vector.scalar_tensor_tensor(out=to_t[:, :], in0=unused, scalar=spare[:, 0:1],
                                                      in1=from_t[:, :], op0=ALU.mult, op1=ALU.add))
            chain.settle()
            dve.sem_inc(s["lists_ready"], 1)

            def from_index(i, k):
                nc.vector.tensor_scalar(from_u[k][:, :], from_t[:, bass.ds(i, 1)], 1.0, None,
                                        ALU.mult).then_inc(s["from_ready"], 1)

            def bias_up(i):
                e = dve.value_load(tile_e[0:1, bass.ds(i, 1)], min_val=0, max_val=E - 1)
                for b in range(HB):
                    dve.wait_ge(s["up_ready"], HB * i + b + 1)
                    nc.vector.tensor_tensor(up_ps[b][:, :], up_ps[b][:, :],
                                            b1_bc[:, bass.ds(e, 1), bass.ts(b, BANK)], ALU.add
                                            ).then_inc(s["biased"], 1)

            def hT_copy(i):
                dve.wait_ge(s["hid_turned"], 2 * i + 2)
                nc.vector.tensor_copy(hT[:, BANK:2 * BANK], turn_ps[1][:, :]).then_inc(s["hT1_ready"], 1)

            def weigh(i, k, chained):
                e = dve.value_load(tile_e[0:1, bass.ds(i, 1)], min_val=0, max_val=E - 1)
                dve.wait_ge(s["yt_free"], i + 1)
                nc.vector.tensor_scalar(to_u[k][:, :], to_t[:, bass.ds(i, 1)], 1.0, None,
                                        ALU.mult).then_inc(s["to_ready"], 1)
                dve.wait_ge(s["down_ready"], i + 1)
                chained.then(nc.vector.tensor_tensor(yt[:, k, :], down_ps[:, 0:C], b2_bc[:, bass.ds(e, 1), :], ALU.add))
                chained.settle()
                nc.vector.tensor_scalar(yt[:, k, :], yt[:, k, :], gate_t[:, bass.ds(i, 1)], None,
                                        ALU.mult).then_inc(s["yt_ready"], 1)

            from_index(0, 0)
            from_index(1, 1)
            dve.wait_ge(s["bias_in"], 32)
            bias_up(0)
            dve.wait_ge(x_in[0], 16)
            from_index(2, 0)
            with dve.Fori(0, (TILES - 3) // 2) as m:
                chain.enter(m, 2)
                for k in range(2):
                    i = 2 * m + k
                    dve.wait_ge(x_in[1 - k], 16 * m + 16 + 16 * k)
                    from_index(i + 3, 1 - k)
                    hT_copy(i)
                    bias_up(i + 1)
                    weigh(i, k, chain)
                chain.leave((TILES - 3) // 2)
            for i in range(TILES - 3, TILES):
                hT_copy(i)
                if i + 1 < TILES:
                    bias_up(i + 1)
                weigh(i, i % 2, chain)

        @block.tensor
        def _(pe):
            def mm(dst, lhsT, rhs, first=True, last=True):
                return nc.tensor.matmul(dst, lhsT, rhs, start=first, stop=last)

            pe.wait_ge(s["setup_done"], 3)
            pe.wait_ge(s["rows_clear"], 3)
            pe.wait_ge(s["weights_in"], 16 * LOADS)

            def turn_rows(g):
                if not (isinstance(g, int) and g == 0):
                    pe.wait_ge(s["zgate_ready"], g * ND)
                pe.wait_ge(s["xn_ready"], g * GT + GT)
                for c in range(KC):
                    for j in range(GT):
                        ins = nc.tensor.transpose(turned_ps[c][:, bass.ts(j, P)], xn4[:, j, bass.ts(c, P)], ident[:, :])
                    ins.then_inc(s["in_ready"], 1)

            def inputs(g, gate):
                later = not (isinstance(g, int) and g == 0)
                for d in range(ND):
                    bank = z_ps[d] if gate else x_ps[d]
                    if gate and later:
                        pe.wait_ge(s["step_read"], 1 + (g - 1) * ND + d + 1)
                    if not gate and d == 0:
                        pe.wait_ge(s["xnT_ready"], g * KC + KC)
                    if not gate and later and d == ND - 1:
                        pe.wait_ge(s["proj_ready"], g)
                    for c in range(KC):
                        ins = mm(bank[:, :], win_sb[:, c, bass.ts(ND * gate + d, P)], xnT[:, c, :],
                                 c == 0, c == KC - 1)
                    ins.then_inc(s["in_ready"], 1)

            def project(g):
                pe.wait_ge(s["xconv_ready"], 1 + g * ND + ND)
                for d in range(ND):
                    ins = mm(proj_ps[:, :], wxp_sb[:, d, :], xconv[:, g, d, :], d == 0, d == ND - 1)
                ins.then_inc(s["step_ready"], 1)

            def steps(g):
                pe.wait_ge(s["proj_ready"], g + 1)
                pe.wait_ge(s["zgate_ready"], g * ND + ND)
                for j in range(GT):
                    ins = nc.tensor.transpose(bturn_ps[:, bass.ts(j, P)], projT[:, bass.ts(j, P)], ident[:, :])
                ins.then_inc(s["b_turned"], 1)
                for d in range(ND):
                    if d == ND - 1:
                        pe.wait_ge(s["bT_ready"], g + 1)
                    mm(step_ps[d][:, :], wdt_sb[0:R, bass.ts(d, P)], projT[0:R, :]
                       ).then_inc(s["step_ready"], 1)

            turn_rows(0)
            inputs(0, False)
            inputs(0, True)
            with pe.Fori(1, NG) as g:
                turn_rows(g)
                project(g - 1)
                inputs(g, False)
                steps(g - 1)
                inputs(g, True)
            project(NG - 1)
            steps(NG - 1)

            pe.sem_inc(s["wT_used"], 1)
            pe.sem_inc(s["g_used"], ND)
            pe.wait_ge(s["dt_ready"], 1 + NG * ND // 2)
            pe.wait_ge(s["dt2_ready"], 1 + NG * ND // 2)
            pe.wait_ge(s["split_ready"], 1 + 2 * NG)

            def b_row(g, n):
                if not (isinstance(g, int) and g == 0 and n < 2):
                    pe.wait_ge(s["dbu_ready"], 1 + (g * NS + n - 1) * NR)
                mm(b_ps[n % 2][:, :], pick_b[:, n:n + 1].broadcast_to([P, P]),
                   proj_hl[:, g, :]).then_inc(s["b_ready"], 1)

            def turn_inputs(g):
                pe.wait_ge(s["dtu_ready"], g * ND + NT)
                pe.wait_ge(s["scan_ready"], ASL + g * NS * ND)
                for b in range(NT):
                    for j in range(GT):
                        ins = nc.tensor.transpose(dbt_ps[b][:, bass.ts(j, P)], dtu[:, NR + b, bass.ts(j, P)],
                                                  ident[:, :])
                    ins.then_inc(s["dtu_turned"], 1)

            def turn_back(q, b):
                pe.wait_ge(s["wT_ready"], GT * q + GT)
                pe.wait_ge(s["scan_ready"], ASL + (q - 1) * ND + NR + b + 1)
                for j in range(GT):
                    ins = nc.tensor.transpose(dbt_ps[b][:, bass.ts(j, P)], wT[:, j, bass.ts(b, P)],
                                              ident[:, :])
                ins.then_inc(s["dbt_ready"], 1)
                if b == NT - 1:
                    pe.wait_ge(s["dbt_ready"], q * NT + NT)
                    pe.sem_inc(s["wT_used"], 1)

            def y_add(g, n, turned=True):
                for d in range(ND):
                    if turned and d >= NR:
                        turn_back(g * NS + n + 1, d - NR)
                    if n == 0 and not (isinstance(g, int) and g == 0):
                        pe.wait_ge(s["y_read"], (g - 1) * ND + d + 1)
                    pe.wait_ge(s["g_ready"], ND + (g * NS + n) * ND + d + 1)
                    mm(y_ps[d][:, :], ident[:, :], g_buf[:, d, :], n == 0, n == NS - 1).then_inc(s["g_used"], 1)

            def y_tell(g):
                for d in range(ND):
                    pe.wait_ge(s["g_used"], ND + (g * NS + NS - 1) * ND + d + 1)
                    pe.sem_inc(s["y_ready"], 1)

            def mix(g, half):
                if half == 0:
                    pe.wait_ge(s["yg_ready"], 1 + g * ND + ND)
                    pe.wait_ge(s["logits_read"], 1 + g)
                else:
                    pe.wait_ge(s["h2_ready"], g * GT + 2)
                for j in (2 * half, 2 * half + 1):
                    for d in range(ND):
                        ins = mm(o_ps[:, bass.ts(j % 2, C)], yg[:, d, bass.ts(j, P)], wout_sb[:, d, :],
                                 d == 0, d == ND - 1)
                ins.then_inc(s["mix_ready"], 1)

            def turn(g, half):
                if half == 0:
                    pe.wait_ge(s["x2_ready"], g * GT + GT)
                else:
                    pe.wait_ge(s["x2T_ready"], 2 * g + 1)
                for j in (2 * half, 2 * half + 1):
                    for c in range(KC):
                        ins = nc.tensor.transpose(o_ps[:, bass.ts((j % 2) * KC + c, P)], x2[:, j, bass.ts(c, P)],
                                                  ident[:, :])
                ins.then_inc(s["x2_turned"], 1)

            def logits(g):
                pe.wait_ge(s["x2T_ready"], 2 * g + 2)
                for j in range(GT):
                    for c in range(KC):
                        ins = mm(o_ps[:, bass.ts(j, E)], x2T[:, bass.ts(j * KC + c, P)], router_sb[:, c, :],
                                 c == 0, c == KC - 1)
                ins.then_inc(s["logits_ready"], 1)

            def scan_group(g, post, last=False):
                turn_inputs(g)
                for b in range(NT):
                    turn_back(g * NS, b)
                for n in range(NS):
                    if n + 2 < NS:
                        b_row(g, n + 2)
                    elif not last:
                        b_row(g + 1, n + 2 - NS)
                    y_add(g, n, n + 1 < NS)
                    if post and n == MIX0:
                        mix(g - 1, 0)
                    if post and n == MIX1:
                        mix(g - 1, 1)
                    if post and n == TURN0:
                        turn(g - 1, 0)
                    if post and n == TURN1:
                        turn(g - 1, 1)
                    if post and n == TURN2:
                        logits(g - 1)
                y_tell(g)

            b_row(0, 0)
            b_row(0, 1)
            scan_group(0, False)
            with pe.Fori(1, NG - 1) as g:
                scan_group(g, True)
            scan_group(NG - 1, True, True)
            mix(NG - 1, 0)
            mix(NG - 1, 1)
            turn(NG - 1, 0)
            turn(NG - 1, 1)
            logits(NG - 1)

            pe.wait_ge(s["hot_ready"], 1)
            mm(rank_ps[:, 0:SEQS * E], before[:, :], hot.rearrange("p i e -> p (i e)"))
            mm(count_ps[:, 0:SEQS * E], ones[:, :], hot.rearrange("p i e -> p (i e)")).then_inc(s["ranks_ready"], 1)
            for r in range(TOPK * SEQS):
                pe.wait_ge(s["onehots_ready"], r + 1)
                ins = mm(order_ps[:, 0:3 * TILES], hot_b[:, r, :], to_add[:, r, :, :].rearrange("p a t -> p (a t)"),
                         r == 0, r == TOPK * SEQS - 1)
            ins.then_inc(s["order_ready"], 1)
            pe.wait_ge(s["lists_ready"], 1)

            def turn_x(i, k, m):
                pe.wait_ge(x_in[k], 16 * m + 16)
                pe.wait_ge(s["xT_ready"], 1 + i)
                for c in range(KC):
                    ins = nc.tensor.transpose(xturn_ps[:, bass.ts(c, P)], xt[:, k, bass.ts(c, P)], ident[:, :])
                ins.then_inc(s["xt_turned"], 1)

            def up(i):
                e = pe.value_load(tile_e[0:1, bass.ds(i, 1)], min_val=0, max_val=E - 1)
                pe.wait_ge(s["experts_ready"], e + 1)
                pe.wait_ge(s["xT_ready"], 1 + i + 1)
                for b in range(HB):
                    for c in range(KC):
                        ins = mm(up_ps[b][:, :], xT[:, bass.ts(c, P)],
                                 w1_sb[:, bass.ds(e, 1), c, bass.ts(b, BANK)], c == 0, c == KC - 1)
                    ins.then_inc(s["up_ready"], 1)

            def turn_h(i):
                for b in range(2):
                    pe.wait_ge(s["hact_ready"], HB * i + b + 1)
                    pe.wait_ge(s[("hT0_ready", "hT1_ready")[b]], 1 + i)
                    for j in range(4):
                        ins = nc.tensor.transpose(turn_ps[b][:, bass.ts(j, P)], hact[:, bass.ts(4 * b + j, P)],
                                                  ident[:, :])
                    ins.then_inc(s["hid_turned"], 1)

            def down(i):
                e = pe.value_load(tile_e[0:1, bass.ds(i, 1)], min_val=0, max_val=E - 1)
                pe.wait_ge(s["yt_ready"], 1 + i)
                pe.wait_ge(s["hT0_ready"], 1 + i + 1)
                pe.wait_ge(s["hT1_ready"], 1 + i + 1)
                for h in range(KH):
                    ins = mm(down_ps[:, 0:C], hT[:, bass.ts(h, P)], w2_sb[:, bass.ds(e, 1), h, :],
                             h == 0, h == KH - 1)
                ins.then_inc(s["down_ready"], 1)

            turn_x(0, 0, 0)
            up(0)
            turn_x(1, 1, 0)
            with pe.Fori(0, (TILES - 3) // 2) as m:
                for k in range(2):
                    i = 2 * m + k
                    turn_h(i)
                    up(i + 1)
                    turn_x(i + 2, k, m + 1)
                    down(i)
            for i in range(TILES - 3, TILES):
                turn_h(i)
                if i + 1 < TILES:
                    up(i + 1)
                if i + 2 < TILES:
                    turn_x(i + 2, i % 2, i // 2 + 1)
                down(i)


def kernel(x, L0_tok_embedding, L0_attn_ln_w, L0_attn_ln_b, L0_attn_W_in, L0_attn_conv_w, L0_attn_conv_b,
           L0_attn_W_xproj, L0_attn_W_dt, L0_attn_b_dt, L0_attn_A_log, L0_attn_Dskip, L0_attn_W_out,
           L0_ffn_router_w, L0_ffn_w1, L0_ffn_b1, L0_ffn_w2, L0_ffn_b2):
    import numpy as _np
    import concourse.bacc as _bacc
    from concourse import mybir as _mybir
    from concourse.bass_utils import run_bass_kernel_spmd as _run

    given = {
        "ids": x.T, "embedding": L0_tok_embedding, "ln_w": L0_attn_ln_w, "ln_b": L0_attn_ln_b,
        "w_in": L0_attn_W_in.T, "conv_w": L0_attn_conv_w, "conv_b": L0_attn_conv_b,
        "w_xproj": L0_attn_W_xproj.T, "w_dt": L0_attn_W_dt.T, "b_dt": L0_attn_b_dt, "a_log": L0_attn_A_log,
        "d_skip": L0_attn_Dskip, "w_out": L0_attn_W_out.T, "router": L0_ffn_router_w.T,
        "w1": L0_ffn_w1.transpose(0, 2, 1), "b1": L0_ffn_b1, "w2": L0_ffn_w2.transpose(0, 2, 1), "b2": L0_ffn_b2,
    }
    nc = _bacc.Bacc("TRN2", target_bir_lowering=False, num_devices=1)
    arrays, args = {}, []
    for name, a in given.items():
        a = _np.ascontiguousarray(a)
        arrays[f"in_{name}"] = a
        args.append(nc.dram_tensor(f"in_{name}", a.shape, _mybir.dt.from_np(a.dtype), kind="ExternalInput").ap())
    seqs, length = x.shape
    shape = (seqs, length, L0_tok_embedding.shape[1])
    args.append(nc.dram_tensor("out", shape, _mybir.dt.float32, kind="ExternalOutput").ap())
    tower_kernel(nc, *args)
    r = _run(nc, [arrays], core_ids=[0])
    return r.results[0]["out"]
```
